# Optimizing a Trainium2 kernel written in Bass

```python
import numpy as np
import jax
import jax.numpy as jnp

def _softmax(x, axis=-1):
    return jax.nn.softmax(x, axis=axis)

def _gelu(x):
    return jax.nn.gelu(x, approximate=True)

def _silu(x):
    return jax.nn.silu(x)

def _sigmoid(x):
    return jax.nn.sigmoid(x)

def _layernorm(x, axis=-1, eps=1e-05):
    m = jnp.mean(x, axis=axis, keepdims=True)
    v = jnp.var(x, axis=axis, keepdims=True)
    return (x - m) / jnp.sqrt(v + eps)

def _scatter_add(tgt, idx, src, axis=0):
    return tgt.at[idx].add(src)

def _segment_sum(src, seg, n):
    return jax.ops.segment_sum(src, seg, n)
kernel_name = 'mk_adaln_d1_jaxref_r2_1b9895'

def setup_inputs(seed: int=0):
    np.random.seed(seed)
    _w = jnp.asarray

    def _L0_attn_setup():
        import jax, jax.numpy as jnp
        import numpy as np
        B, T, C, H = (2, 512, 512, 16)
        D = C // H
        EPS = 1e-06
        key = jax.random.key(seed)
        k1, k2, k3, k4, k5 = jax.random.split(key, 5)
        s = 0.02
        return {'x': jax.random.normal(k1, (B, T, C), dtype=jnp.float32), 'w_qkv': jax.random.normal(k2, (3 * C, C), dtype=jnp.float32) * s, 'b_qkv': jax.random.normal(k3, (3 * C,), dtype=jnp.float32) * s, 'w_out': jax.random.normal(k4, (C, C), dtype=jnp.float32) * s, 'b_out': jax.random.normal(k5, (C,), dtype=jnp.float32) * s}
    _L0_attn_in = _L0_attn_setup()

    def _L0_ffn_setup():
        import jax, jax.numpy as jnp
        import numpy as np
        DIM = 512
        HIDDEN = 1536
        SCALE = 1.0 / 127.0

        def _dequant(w_int, dtype):
            return w_int.astype(dtype) * jnp.asarray(SCALE, dtype)
        key = jax.random.key(seed)
        k_x, k_g, k_u, k_d = jax.random.split(key, 4)
        x = jax.random.normal(k_x, (4, 1024, DIM), dtype=jnp.float32)
        w_gate = jax.random.randint(k_g, (HIDDEN, DIM), -127, 128, dtype=jnp.int32)
        w_up = jax.random.randint(k_u, (HIDDEN, DIM), -127, 128, dtype=jnp.int32)
        w_down = jax.random.randint(k_d, (DIM, HIDDEN), -127, 128, dtype=jnp.int32)
        return {'x': x, 'w_gate': w_gate, 'w_up': w_up, 'w_down': w_down}
    _L0_ffn_in = _L0_ffn_setup()
    _L0_c = _w((lambda *s: np.random.randn(*s).astype(np.float32) * 0.05)(1, 512))
    _L0_wmod = _w((lambda *s: np.random.randn(*s).astype(np.float32) * 0.05)(512, 6 * 512) * 512 ** (-0.5))
    _d = {'L0_attn_x': _L0_attn_in['x'], 'L0_attn_w_qkv': _L0_attn_in['w_qkv'], 'L0_attn_b_qkv': _L0_attn_in['b_qkv'], 'L0_attn_w_out': _L0_attn_in['w_out'], 'L0_attn_b_out': _L0_attn_in['b_out'], 'L0_ffn_w_gate': _L0_ffn_in['w_gate'], 'L0_ffn_w_up': _L0_ffn_in['w_up'], 'L0_ffn_w_down': _L0_ffn_in['w_down'], 'L0_c': _L0_c, 'L0_wmod': _L0_wmod}
    _x0 = _d['L0_attn_x']
    _d['L0_attn_x'] = jax.random.normal(jax.random.fold_in(jax.random.key(seed), 1), (1, 8192, 512), dtype=_x0.dtype)
    del _x0
    return _d

def reference(L0_attn_x, L0_attn_w_qkv, L0_attn_b_qkv, L0_attn_w_out, L0_attn_b_out, L0_ffn_w_gate, L0_ffn_w_up, L0_ffn_w_down, L0_c, L0_wmod):

    def _L0_attn_ref(x, w_qkv, b_qkv, w_out, b_out):
        import jax, jax.numpy as jnp
        import numpy as np
        B, T, C, H = (2, 512, 512, 16)
        D = C // H
        EPS = 1e-06
        b, t, c = x.shape
        qkv = x @ w_qkv.T + b_qkv
        q, k, v = jnp.split(qkv, 3, axis=-1)

        def to_heads(u):
            return u.reshape(b, t, H, D).transpose(0, 2, 1, 3).astype(jnp.float32)
        q, k, v = (to_heads(q), to_heads(k), to_heads(v))
        q_prime = jax.nn.elu(q) + 1.0
        k_prime = jax.nn.elu(k) + 1.0
        kv_cumsum = jnp.cumsum(jnp.einsum('bhtd,bhte->bhtde', k_prime, v), axis=2)
        context = jnp.einsum('bhtd,bhtde->bhte', q_prime, kv_cumsum)
        norm = jnp.einsum('bhtd,bhtd->bht', q_prime, jnp.cumsum(k_prime, axis=2))
        out = context / (norm[..., None] + EPS)
        out = out.astype(x.dtype).transpose(0, 2, 1, 3).reshape(b, t, c)
        return out @ w_out.T + b_out

    def _L0_ffn_ref(x, w_gate, w_up, w_down):
        import jax, jax.numpy as jnp
        import numpy as np
        DIM = 512
        HIDDEN = 1536
        SCALE = 1.0 / 127.0

        def _dequant(w_int, dtype):
            return w_int.astype(dtype) * jnp.asarray(SCALE, dtype)
        wg = _dequant(w_gate, x.dtype)
        wu = _dequant(w_up, x.dtype)
        wd = _dequant(w_down, x.dtype)
        gate = jnp.einsum('bsd,hd->bsh', x, wg)
        up = jnp.einsum('bsd,hd->bsh', x, wu)
        h = jax.nn.silu(gate) * up
        return jnp.einsum('bsh,dh->bsd', h, wd)
    x = L0_attn_x
    mod = (_silu(L0_c) @ L0_wmod).reshape(L0_c.shape[0], 6, 1, -1)
    sa, ca, ga, sb, cb, gb = (mod[:, 0], mod[:, 1], mod[:, 2], mod[:, 3], mod[:, 4], mod[:, 5])
    ga = (2 * (ga >= 0) - 1) * jnp.maximum(jnp.abs(ga), 0.25)
    gb = (2 * (gb >= 0) - 1) * jnp.maximum(jnp.abs(gb), 0.25)
    h = _layernorm(x, axis=-1) * (1 + ca) + sa
    x = x + ga * _L0_attn_ref(h, L0_attn_w_qkv, L0_attn_b_qkv, L0_attn_w_out, L0_attn_b_out)
    h = _layernorm(x, axis=-1) * (1 + cb) + sb
    x = x + gb * _L0_ffn_ref(h, L0_ffn_w_gate, L0_ffn_w_up, L0_ffn_w_down)
    return x

_drawn_inputs = setup_inputs


def setup_inputs(seed=0):
    import zlib

    import numpy as np

    out = dict(_drawn_inputs(seed))
    spreads = {}
    factors = {'L0_attn_w_qkv': 8.0, 'L0_attn_b_qkv': 8.0, 'L0_attn_w_out': 8.0, 'L0_attn_b_out': 8.0}
    for name, (base, spread) in spreads.items():
        noise = np.random.default_rng([zlib.crc32(name.encode()), seed]).standard_normal(out[name].shape)
        drawn = base * np.exp(spread * noise) if base else spread * noise
        out[name] = jnp.asarray(drawn.astype(out[name].dtype))
    for name, factor in factors.items():
        out[name] = (out[name] * factor).astype(out[name].dtype)
    return out
```

```python
from contextlib import ExitStack

import concourse.bass as bass
from concourse import mybir

F32 = mybir.dt.float32
F32R = mybir.dt.float32r
I32 = mybir.dt.int32
ALU = mybir.AluOpType
ACT = mybir.ActivationFunctionType

P = 128
HD = 32
HG = P // HD
HV = HD + 1
LN_EPS = 1e-5
ATTN_EPS = 1e-6
W_SCALE = 1.0 / 127.0


def adaln_block(nc, x, wqkv_t, b_qk, b_v, wout_t, b_out, wg_t, wu_t, wd_t, c_in, wmod, out):
    T, C = x.shape
    F = wg_t.shape[1]
    KC = C // P
    KF = F // P
    H = C // HD
    GV = HG * HV
    CH = P
    TB = 2 * CH
    NB = T // TB
    NT = 4
    FB = NT * P
    NF = T // FB
    assert NB % 2 == 0 and NB >= 6 and NF % 2 == 0 and KC == 4 and KF % 2 == 0

    TURN_AT = KF - 4
    turn_bank = (6, 7, 4, 5)
    x_blocks = x.rearrange("(n t p) c -> n p t c", p=P, t=2)
    x_chunks = x.rearrange("(n p) c -> n p c", p=P)
    x1_dram = nc.dram_tensor("x1_dram", (T, C), F32, kind="Internal").ap()
    x1_chunks = x1_dram.rearrange("(n p) c -> n p c", p=P)
    x1_blocks = x1_dram.rearrange("(n t p) c -> n p t c", p=P, t=NT)
    out_blocks = out.rearrange("(n t p) c -> n p t c", p=P, t=NT)

    with ExitStack() as ctx:
        def sem(name):
            return ctx.enter_context(nc.semaphore(name))

        base = (nc.sbuf_base + 63) // 64 * 64
        top = [base]

        def at(name, shape, dtype, offset):
            return nc.alloc_sbuf_tensor_at(name, shape, dtype, offset=offset)

        def sb(name, shape, dtype):
            n = 4
            for s in shape[1:]:
                n *= s
            t = at(name, shape, dtype, top[0])
            top[0] += (n + 31) // 32 * 32
            return t

        ident = sb("ident", (P, P), F32)
        mod_cols = sb("mod_cols", (P, 4 * KC), F32)
        gb_rows = sb("gb_rows", (P, C), F32)
        neg_half = sb("neg_half", (P, NT), F32)
        eps_cols = sb("eps_cols", (P, NT), F32)
        wait_pad = sb("wait_pad", (P, 1), F32)
        mean_var = sb("mean_var", (P, NT, 2), F32)
        var_eps = sb("var_eps", (P, NT), F32)
        rstd = sb("rstd", (P, NT), F32)
        bn = sb("bn", (P, NT, 6), F32)
        wqkv_at = top[0]
        wqkv_h = sb("wqkv_h", (P, KC, 3 * C), F32R)
        wqkv_l = sb("wqkv_l", (P, KC, 3 * C), F32R)
        wu = at("wu", (P, KC, F), F32R, wqkv_at)
        wd = at("wd", (P, KF, C), F32R, wqkv_at + KC * F * 4)
        wout_h = sb("wout_h", (P, KC, C), F32R)
        wout_l = sb("wout_l", (P, KC, C), F32R)
        stage_at = top[0]
        stage_w = sb("stage_w", (P, KC, 3 * C), F32)
        stage_m = sb("stage_m", (P, KC, 2 * C), F32)
        wg = at("wg", (P, KC, F), F32R, stage_at)
        qpad_h = at("qpad_h", (P, KC, HG, CH), F32R, stage_at + KC * F * 4)
        qpad_l = at("qpad_l", (P, KC, HG, CH), F32R, stage_at + (KC * F + KC * HG * CH) * 4)
        assert KC * F + 2 * KC * HG * CH <= (top[0] - stage_at) // 4
        phase1_at = top[0]
        xb = sb("xb", (P, 2, 2, C), F32)
        xn = sb("xn", (P, 2, C), F32)
        hf = sb("hf", (P, KC, TB), F32)
        hh = sb("hh", (P, KC, TB), F32R)
        hl = sb("hl", (P, KC, TB), F32R)
        e_part = sb("e_part", (P, 2, 2, TB), F32)
        r_part = sb("r_part", (P, 2, 2, TB), F32)
        early_end = top[0]
        qk = sb("qk", (P, 2, KC, 2, TB), F32)
        k_rows = sb("k_rows", (P, 2, 2, KC, P), F32)
        v_rows = sb("v_rows", (P, 2, 2, H * HV), F32)
        k_h = sb("k_h", (P, KC, CH), F32R)
        k_l = sb("k_l", (P, KC, CH), F32R)
        masked = sb("masked", (P, KC, HG, CH), F32)
        state = sb("state", (P, KC, GV), F32)
        ctx_rows = sb("ctx_rows", (P, C), F32)
        den = sb("den", (P, H), F32)
        rden = sb("rden", (P, H), F32)
        ctx_h = sb("ctx_h", (P, 2, KC, CH), F32R)
        ctx_l = sb("ctx_l", (P, 2, KC, CH), F32R)
        xres = sb("xres", (P, 2, C), F32)
        causal = sb("causal", (P, CH), F32)
        head_mask = sb("head_mask", (P, GV), F32)
        bqk_cols = sb("bqk_cols", (P, 2 * KC), F32)
        neg_bqk_cols = sb("neg_bqk_cols", (P, 2 * KC), F32)
        bv_rows = sb("bv_rows", (P, C), F32)
        gab_rows = sb("gab_rows", (P, C), F32)
        c_cols = sb("c_cols", (P, KC), F32)
        silu_c = sb("silu_c", (P, KC), F32)
        ones_row = sb("ones_row", (P, P), F32)
        silu_wide = ctx_rows[:].rearrange("p (k q) -> p k q", k=KC)
        ga_rows, sgn_rows, abs_rows = (masked[:, j].rearrange("p g t -> p (g t)") for j in (1, 2, 3))
        print("sbuf used", top[0], "of", nc.sbuf_usable_end)
        assert top[0] <= nc.sbuf_usable_end
        top[0] = phase1_at
        x1b = [sb("x1b0", (P, NT, C), F32), None]
        x1n = sb("x1n", (P, NT, C), F32)
        g_hl = [[None, None], [None, None]]
        g_hl[0][0] = sb("g_h0", (P, KC, FB), F32R)
        g_hl[0][1] = sb("g_l0", (P, KC, FB), F32R)
        assert top[0] <= early_end
        x1b[1] = sb("x1b1", (P, NT, C), F32)
        g_hl[1][0] = sb("g_h1", (P, KC, FB), F32R)
        g_hl[1][1] = sb("g_l1", (P, KC, FB), F32R)
        gf = sb("gf", (P, 2, FB), F32)
        sil = sb("sil", (P, 2, FB), F32)
        hid = sb("hid", (P, 2, FB), F32)
        hid_h = sb("hid_h", (P, 4, FB), F32R)
        hid_l = sb("hid_l", (P, 4, FB), F32R)
        y = sb("y", (P, NT, C), F32)
        assert top[0] <= nc.sbuf_usable_end

        bank = [ctx.enter_context(nc.psum_tensor(f"bank{b}", (P, 512), F32)) for b in range(8)]
        state_bank = bank[4:6]
        ring = bank[6:8]

        consts_ready = sem("consts_ready")
        c_loaded = sem("c_loaded")
        biases_loaded = sem("biases_loaded")
        mod1_loaded = sem("mod1_loaded")
        wqkv_loaded = sem("wqkv_loaded")
        wqkv_ready = sem("wqkv_ready")
        silu_ready = sem("silu_ready")
        wide_ready = sem("wide_ready")
        cols_done = sem("cols_done")
        rows_done = sem("rows_done")
        neg_ready = sem("neg_ready")
        cols_ready = sem("cols_ready")
        wout_loaded = sem("wout_loaded")
        mod_ga_loaded = sem("mod_ga_loaded")
        mod2_loaded = sem("mod2_loaded")
        mod_gb_loaded = sem("mod_gb_loaded")
        stage_free = sem("stage_free")
        setup_step = sem("setup_step")
        wout_ready = sem("wout_ready")
        rows_ready = sem("rows_ready")
        state_zeroed = sem("state_zeroed")
        wg_loaded = sem("wg_loaded")
        wu_loaded = sem("wu_loaded")
        wd_loaded = sem("wd_loaded")

        x_loaded = [sem("x_loaded0"), sem("x_loaded1")]
        bn_done = sem("bn_done")
        stats_ready = sem("stats_ready")
        var_ready = sem("var_ready")
        rstd_ready = sem("rstd_ready")
        xn_ready = sem("xn_ready")
        x_turned = sem("x_turned")
        hf_ready = sem("hf_ready")
        hh_ready = sem("hh_ready")
        hl_ready = sem("hl_ready")
        qk_done = sem("qk_done")
        qk_read = sem("qk_read")
        elu_parts = sem("elu_parts")
        qk_ready = sem("qk_ready")
        k_turned = sem("k_turned")
        k_rows_ready = sem("k_rows_ready")
        v_done = sem("v_done")
        v_ready = sem("v_ready")
        pads_cleared = sem("pads_cleared")
        pad_h_ready = sem("pad_h_ready")
        pad_l_ready = sem("pad_l_ready")
        scores_done = sem("scores_done")
        masked_ready = sem("masked_ready")
        context_done = sem("context_done")
        den_ready = sem("den_ready")
        rden_ready = sem("rden_ready")
        ctx_ready = sem("ctx_ready")
        state_done = sem("state_done")
        state_ready = sem("state_ready")
        ctx_turned = sem("ctx_turned")
        ctx_h_ready = sem("ctx_h_ready")
        ctx_l_ready = sem("ctx_l_ready")
        out_done = sem("out_done")
        xres_loaded = [sem("xres_loaded0"), sem("xres_loaded1")]
        xres_ready = sem("xres_ready")
        x1_ready = sem("x1_ready")
        x1_stored = [sem("x1_stored0"), sem("x1_stored1")]

        x1_loaded = [sem("x1_loaded0"), sem("x1_loaded1")]
        f_bn = sem("f_bn")
        f_stats = sem("f_stats")
        f_var = sem("f_var")
        f_rstd = sem("f_rstd")
        f_norm = sem("f_norm")
        f_turned = sem("f_turned")
        f_mod = sem("f_mod")
        f_h = sem("f_h")
        f_l = sem("f_l")
        gu_done = sem("gu_done")
        sil_ready = sem("sil_ready")
        hid_ready = sem("hid_ready")
        hid_h_ready = sem("hid_h_ready")
        hid_l_ready = sem("hid_l_ready")
        down_k = sem("down_k")
        scaled = sem("scaled")
        y_ready = sem("y_ready")
        y_stored = sem("y_stored")

        block = ctx.enter_context(nc.Block())

        def phase1_blocks(eng, step):
            step(0, 0, 0, True, True, True)
            with eng.Fori(0, (NB - 4) // 2) as j:
                step(2 * j + 1, j, 1, False, True, True)
                step(2 * j + 2, j + 1, 0, False, True, True)
            step(NB - 3, (NB - 4) // 2, 1, False, True, True)
            step(NB - 2, (NB - 2) // 2, 0, False, False, True)
            step(NB - 1, (NB - 2) // 2, 1, False, False, False)

        def phase2_blocks(eng, step):
            step(0, 0, 0, True, True)
            with eng.Fori(0, (NF - 2) // 2) as j:
                step(2 * j + 1, j, 1, False, True)
                step(2 * j + 2, j + 1, 0, False, True)
            step(NF - 1, (NF - 2) // 2, 1, False, False)

        @block.sync
        def _(sp):
            sp.dma_start(c_cols[:], c_in).then_inc(c_loaded, 16)
            sp.dma_start(bqk_cols[:], b_qk).then_inc(biases_loaded, 16)
            sp.dma_start(bv_rows[:], b_v.partition_broadcast(P)).then_inc(biases_loaded, 16)
            sp.dma_start(gab_rows[:], b_out.partition_broadcast(P)).then_inc(biases_loaded, 16)
            sp.dma_start(xb[:, 0], x_blocks[0]).then_inc(x_loaded[0], 16)
            sp.dma_start(stage_m[:], wmod.rearrange("(k p) n -> p k n", p=P)[:, :, 0:2 * C])\
              .then_inc(mod1_loaded, 16)
            sp.dma_start(stage_w[:], wqkv_t.rearrange("(k p) n -> p k n", p=P)).then_inc(wqkv_loaded, 16)
            sp.dma_start(xb[:, 1], x_blocks[1]).then_inc(x_loaded[1], 16)
            sp.wait_ge(stage_free, 1)
            sp.dma_start(stage_w[:, :, 0:C], wout_t.rearrange("(k p) n -> p k n", p=P)).then_inc(wout_loaded, 16)
            sp.dma_start(stage_w[:, :, C:2 * C], wmod.rearrange("(k p) n -> p k n", p=P)[:, :, 2 * C:3 * C])\
              .then_inc(mod_ga_loaded, 16)
            sp.dma_start(stage_w[:, :, 2 * C:3 * C], wmod.rearrange("(k p) n -> p k n", p=P)[:, :, 5 * C:6 * C])\
              .then_inc(mod_gb_loaded, 16)
            sp.wait_ge(cols_done, 1)
            sp.dma_start(stage_m[:], wmod.rearrange("(k p) n -> p k n", p=P)[:, :, 3 * C:5 * C])\
              .then_inc(mod2_loaded, 16)

            def store_x1(chunk, c):
                sp.wait_ge(x1_ready, chunk + 1)
                sp.dma_start(x1_chunks[chunk], xres[:, c]).then_inc(x1_stored[c], 16)

            def step(i, half, parity, first, has_x, has_proj):
                if has_x:
                    sp.wait_ge(xn_ready, 2 * i + 2)
                    sp.dma_start(xb[:, parity], x_blocks[i + 2]).then_inc(x_loaded[parity], 16)
                if not has_proj:
                    sp.wait_ge(xn_ready, 2 * NB)
                    sp.dma_start(x1b[0][:], x1_blocks[0]).then_inc(x1_loaded[0], 16)
                for c in range(2):
                    if not first:
                        sp.wait_ge(x1_stored[c], 16 * i)
                    sp.dma_start(xres[:, c], x_chunks[2 * i + c]).then_inc(xres_loaded[c], 16)
                    if c == 1:
                        store_x1(2 * i, 0)
                    elif not first:
                        store_x1(2 * i - 1, 1)

            phase1_blocks(sp, step)
            store_x1(2 * NB - 1, 1)

            sp.wait_ge(x1_stored[0], 16 * NB)
            sp.wait_ge(x1_stored[1], 16 * NB)
            sp.dma_start(x1b[1][:], x1_blocks[1]).then_inc(x1_loaded[1], 16)

            def fstep(b, half, parity, first, has_next):
                sp.wait_ge(y_ready, NT * b + NT)
                sp.dma_start(out_blocks[b], y[:]).then_inc(y_stored, 16)

            def fstep_load(b, parity):
                sp.dma_start(x1b[parity][:], x1_blocks[b + 2]).then_inc(x1_loaded[parity], 16)

            fstep(0, 0, 0, True, True)
            fstep_load(0, 0)
            with sp.Fori(0, (NF - 4) // 2) as j:
                fstep(2 * j + 1, j, 1, False, True)
                fstep_load(2 * j + 1, 1)
                fstep(2 * j + 2, j + 1, 0, False, True)
                fstep_load(2 * j + 2, 0)
            fstep(NF - 3, None, 1, False, True)
            fstep_load(NF - 3, 1)
            fstep(NF - 2, None, 0, False, True)
            fstep(NF - 1, None, 1, False, False)
            sp.wait_ge(y_stored, 16 * NF)

        @block.gpsimd
        def _(pool):
            pool.memset(ident[:], 0.0)
            pool.memset(causal[:], 1.0)
            pool.memset(neg_half[:], -0.5)
            pool.memset(eps_cols[:], LN_EPS)
            pool.memset(ones_row[:], 1.0)
            pool.memset(v_rows[:], 1.0)
            pool.memset(masked[:, 0], 0.0).then_inc(consts_ready, 1)
            pool.wait_ge(consts_ready, 1)
            pool.affine_select(out=ident[:], in_=ident[:], compare_op=ALU.not_equal, fill=1.0, base=0,
                               pattern=[[-1, P]], channel_multiplier=1)
            pool.affine_select(out=causal[:], in_=causal[:], compare_op=ALU.is_ge, fill=0.0, base=0,
                               pattern=[[1, CH]], channel_multiplier=-1).then_inc(consts_ready, 1)

            def rstd_of(m):
                pool.wait_ge(stats_ready, 2 * m + 2)
                pool.tensor_tensor(var_eps[:, 0:2], mean_var[:, 0:2, 1], eps_cols[:, 0:2], ALU.add).then_inc(var_ready, 1)
                pool.wait_ge(var_ready, m + 1)
                pool.tensor_tensor(rstd[:, 0:2], var_eps[:, 0:2], neg_half[:, 0:2], ALU.pow).then_inc(rstd_ready, 1)

            def residual(chunk, loads, c):
                pool.wait_ge(xres_loaded[c], 16 * loads)
                pool.tensor_tensor(xres[:, c], xres[:, c], gab_rows[:], ALU.add).then_inc(xres_ready, 1)

            rstd_of(0)
            rstd_of(1)
            pool.wait_ge(rows_ready, 1)
            pool.dma_start(wg[:], wg_t.rearrange("(k p) n -> p k n", p=P)).then_inc(wg_loaded, 16)

            def step(i, half, parity, first, has_x, has_proj):
                if not has_proj:
                    pool.wait_ge(v_done, 2 * NB)
                    pool.dma_start(wu[:], wu_t.rearrange("(k p) n -> p k n", p=P)).then_inc(wu_loaded, 16)
                    pool.dma_start(wd[:], wd_t.rearrange("(k p) n -> p k n", p=P)).then_inc(wd_loaded, 16)
                residual(2 * i, i + 1, 0)
                if has_x:
                    rstd_of(i + 2)
                residual(2 * i + 1, i + 1, 1)

            phase1_blocks(pool, step)

            def f_rstd_of(b):
                pool.wait_ge(f_stats, NT * b + NT)
                pool.tensor_tensor(var_eps[:], mean_var[:, :, 1], eps_cols[:], ALU.add).then_inc(f_var, 1)
                pool.wait_ge(f_var, b + 1)
                pool.tensor_tensor(rstd[:], var_eps[:], neg_half[:], ALU.pow).then_inc(f_rstd, 1)

            f_rstd_of(0)
            with pool.Fori(1, NF) as b:
                f_rstd_of(b)

        @block.scalar
        def _(act):
            act.wait_ge(c_loaded, 16)
            act.activation(silu_c[:], c_cols[:], ACT.Silu).then_inc(silu_ready, 1)
            act.wait_ge(cols_ready, 1)

            def turn_in(m):
                for u in range(2):
                    act.wait_ge(x_turned, 2 * m + u + 1)
                    if u == 0:
                        act.wait_ge(hl_ready, 2 * m)
                    for q in range(2):
                        k = 2 * u + q
                        act.activation(hf[:, k], ring[u][:, q * TB:(q + 1) * TB], ACT.Identity,
                                       bias=mod_cols[:, k:k + 1],
                                       scale=mod_cols[:, KC + k:KC + k + 1]).then_inc(hf_ready, 1)

            def turn_in_first():
                for u in range(2):
                    act.wait_ge(x_turned, u + 1)
                    for q in range(2):
                        k = 2 * u + q
                        act.activation(hf[:, k], ring[u][:, q * TB:(q + 1) * TB], ACT.Identity,
                                       bias=mod_cols[:, k:k + 1],
                                       scale=mod_cols[:, KC + k:KC + k + 1]).then_inc(hf_ready, 1)

            def elu(n, g, b):
                act.wait_ge(qk_done, 4 * n + g + 1)
                if g >= 2:
                    act.wait_ge(qk_ready, 4 * n + g - 1)
                for s in range(2):
                    act.activation(e_part[:, g % 2, s], ring[b][:, s * TB:(s + 1) * TB], ACT.Relu,
                                   bias=neg_bqk_cols[:, s * KC + g:s * KC + g + 1], scale=-1.0)
                for s in range(2):
                    last = act.activation(r_part[:, g % 2, s], ring[b][:, s * TB:(s + 1) * TB], ACT.Relu,
                                          bias=bqk_cols[:, s * KC + g:s * KC + g + 1])
                last.then_inc(qk_read, 1)
                act.wait_ge(qk_read, 4 * n + g + 1)
                act.activation(e_part[:, g % 2], e_part[:, g % 2], ACT.Exp, scale=-1.0).then_inc(elu_parts, 1)

            def k_in(n, u, b, parity):
                act.wait_ge(k_turned, 2 * n + u + 1)
                act.activation(k_rows[:, parity, :, 2 * u:2 * u + 2, :],
                               ring[b][:, :].rearrange("p (g c d) -> p c g d", g=2, c=2), ACT.Copy)\
                   .then_inc(k_rows_ready, 1)

            def spread_high(chunk, parity, c):
                for j in range(HG):
                    rows = slice(HD * j, HD * (j + 1))
                    act.activation(qpad_h[rows, :, j], qk[rows, parity, :, 0, c * CH:(c + 1) * CH], ACT.Copy)
                act.activation(k_h[:], qk[:, parity, :, 1, c * CH:(c + 1) * CH], ACT.Copy).then_inc(pad_h_ready, 1)

            def ctx_split(chunk, c, b):
                act.wait_ge(ctx_turned, chunk + 1)
                act.activation(ctx_h[:, c], ring[b][:, :].rearrange("p (k t) -> p k t", k=KC), ACT.Copy)\
                   .then_inc(ctx_h_ready, 1)

            turn_in_first()
            act.wait_ge(biases_loaded, 48)
            act.wait_ge(neg_ready, 1)
            for g in range(4):
                elu(0, g, g % 2)
            k_in(0, 0, 0, 0)
            k_in(0, 1, 1, 0)
            turn_in(1)
            act.wait_ge(pads_cleared, 1)
            act.wait_ge(qk_ready, 4)
            spread_high(0, 0, 0)

            def step(i, half, parity, first, has_x, has_proj):
                if not first:
                    ctx_split(2 * i - 1, 1, 0)
                if has_proj:
                    elu(i + 1, 0, 1)
                act.wait_ge(scores_done, 8 * i + 4)
                spread_high(2 * i + 1, parity, 1)
                if has_proj:
                    elu(i + 1, 1, 0)
                    elu(i + 1, 2, 1)
                    elu(i + 1, 3, 0)
                    k_in(i + 1, 0, 0, 1 - parity)
                ctx_split(2 * i, 0, 1)
                if has_proj:
                    k_in(i + 1, 1, 0, 1 - parity)
                    act.wait_ge(scores_done, 8 * i + 8)
                    act.wait_ge(qk_ready, 4 * i + 8)
                    spread_high(2 * i + 2, 1 - parity, 0)
                if has_x:
                    turn_in(i + 2)

            phase1_blocks(act, step)
            ctx_split(2 * NB - 1, 1, 0)

            def f_turn_in(b, pair):
                for k in (2 * pair, 2 * pair + 1):
                    act.wait_ge(f_turned, KC * b + k + 1)
                    if not (isinstance(b, int) and b == 0 and k < 2):
                        act.wait_ge(f_l, KC * b + k - 1)
                    act.activation(gf[:, k % 2], bank[turn_bank[k]][:], ACT.Identity,
                                   bias=mod_cols[:, 2 * KC + k:2 * KC + k + 1],
                                   scale=mod_cols[:, 3 * KC + k:3 * KC + k + 1]).then_inc(f_mod, 1)

            def silu(b, k):
                act.wait_ge(gu_done, KF * b + k + 1)
                if not (isinstance(b, int) and b == 0 and k < 2):
                    act.wait_ge(hid_ready, KF * b + k - 1)
                act.activation(sil[:, k % 2], bank[4 + 2 * (k % 2)][:], ACT.Silu, scale=W_SCALE)\
                   .then_inc(sil_ready, 1)

            def hid_split(b, k):
                act.wait_ge(hid_ready, KF * b + k + 1)
                if not (isinstance(b, int) and b == 0 and k < 4):
                    act.wait_ge(down_k, KF * b + k - 3)
                act.activation(hid_h[:, k % 4], hid[:, k % 2], ACT.Copy).then_inc(hid_h_ready, 1)

            f_turn_in(0, 0)
            f_turn_in(0, 1)

            def fstep(b, half, parity, first, has_next):
                silu(b, 0)
                for k in range(KF):
                    if k == TURN_AT and has_next:
                        f_turn_in(b + 1, 0)
                        f_turn_in(b + 1, 1)
                    if k + 1 < KF:
                        silu(b, k + 1)
                    hid_split(b, k)

            phase2_blocks(act, fstep)

        @block.vector
        def _(dve):
            def normalise(m, loads, parity):
                dve.wait_ge(x_loaded[parity], 16 * loads)
                for t in range(2):
                    dve.bn_stats(bn[:, t], xb[:, parity, t]).then_inc(bn_done, 1)
                dve.wait_ge(bn_done, 2 * m + 2)
                dve.memset(wait_pad[:], 0.0)
                for t in range(2):
                    dve.bn_aggr(mean_var[:, t], bn[:, t]).then_inc(stats_ready, 1)

            def normalise2(m, parity):
                dve.wait_ge(rstd_ready, m + 1)
                if not (isinstance(m, int) and m == 0):
                    dve.wait_ge(x_turned, 2 * m)
                for t in range(2):
                    dve.tensor_scalar(xn[:, t], xb[:, parity, t], mean_var[:, t, 0:1], rstd[:, t:t + 1],
                                      ALU.subtract, ALU.mult).then_inc(xn_ready, 1)

            def split_h(m):
                if not (isinstance(m, int) and m == 0):
                    dve.wait_ge(v_done, 2 * m)
                for u in range(2):
                    k = slice(2 * u, 2 * u + 2)
                    dve.wait_ge(hf_ready, 4 * m + 2 * u + 2)
                    dve.tensor_copy(hh[:, k], hf[:, k]).then_inc(hh_ready, 1)
                    dve.wait_ge(hh_ready, 2 * m + u + 1)
                    dve.tensor_tensor(hl[:, k], hf[:, k], hh[:, k].bitcast(F32), ALU.subtract).then_inc(hl_ready, 1)

            def elu_sum(n, g, parity):
                dve.wait_ge(elu_parts, 4 * n + g + 1)
                dve.tensor_tensor(qk[:, parity, g], e_part[:, g % 2], r_part[:, g % 2], ALU.add)\
                   .then_inc(qk_ready, 1)

            def values(n, c, parity, b):
                dve.wait_ge(v_done, 2 * n + c + 1)
                dve.tensor_tensor(v_rows[:, parity, c].rearrange("p (h e) -> p h e", e=HV)[:, :, 0:HD],
                                  ring[b][:, :].rearrange("p (h e) -> p h e", e=HD),
                                  bv_rows[:].rearrange("p (h e) -> p h e", e=HD), ALU.add).then_inc(v_ready, 1)

            def mask_scores(chunk):
                for g in range(KC):
                    dve.wait_ge(scores_done, 4 * chunk + g + 1)
                    dve.tensor_tensor(masked[:, g], bank[g][:, :].rearrange("p (j t) -> p j t", j=HG),
                                      causal[:].unsqueeze(1).broadcast_to((P, HG, CH)), ALU.mult)\
                       .then_inc(masked_ready, 1)

            def spread_low(chunk, parity, c):
                dve.wait_ge(pad_h_ready, chunk + 1)
                for j in range(HG):
                    rows = slice(HD * j, HD * (j + 1))
                    dve.tensor_tensor(qpad_l[rows, :, j], qk[rows, parity, :, 0, c * CH:(c + 1) * CH],
                                      qpad_h[rows, :, j].bitcast(F32), ALU.subtract)
                dve.tensor_tensor(k_l[:], qk[:, parity, :, 1, c * CH:(c + 1) * CH], k_h[:].bitcast(F32),
                                  ALU.subtract).then_inc(pad_l_ready, 1)

            def context(chunk):
                dve.wait_ge(context_done, chunk + 1)
                half_h = H // 2
                for u in range(2):
                    rows = bank[u][:, 0:half_h * HV].rearrange("p (h e) -> p h e", e=HV)
                    last = dve.tensor_scalar(den[:, u * half_h:(u + 1) * half_h], rows[:, :, HD], ATTN_EPS, None, ALU.add)
                last.then_inc(den_ready, 1)
                dve.wait_ge(den_ready, chunk + 1)
                dve.reciprocal(rden[:], den[:]).then_inc(rden_ready, 1)
                dve.wait_ge(rden_ready, chunk + 1)
                if not (isinstance(chunk, int) and chunk == 0):
                    dve.wait_ge(ctx_turned, chunk)
                for u in range(2):
                    rows = bank[u][:, 0:half_h * HV].rearrange("p (h e) -> p h e", e=HV)
                    last = dve.tensor_tensor(
                        ctx_rows[:, u * half_h * HD:(u + 1) * half_h * HD].rearrange("p (h e) -> p h e", e=HD),
                        rows[:, :, 0:HD],
                        rden[:, u * half_h:(u + 1) * half_h].unsqueeze(2).broadcast_to((P, half_h, HD)), ALU.mult)
                last.then_inc(ctx_ready, 1)

            def mask_state():
                for u in range(2):
                    last = dve.tensor_tensor(state[:, 2 * u:2 * u + 2],
                                             state_bank[u][:, 0:2 * GV].rearrange("p (g e) -> p g e", g=2),
                                             head_mask[:].unsqueeze(1).broadcast_to((P, 2, GV)), ALU.mult)
                last.then_inc(state_ready, 1)

            def ctx_low(chunk, c, b):
                dve.wait_ge(ctx_h_ready, chunk + 1)
                dve.tensor_tensor(ctx_l[:, c], ring[b][:, :].rearrange("p (k t) -> p k t", k=KC),
                                  ctx_h[:, c].bitcast(F32), ALU.subtract).then_inc(ctx_l_ready, 1)

            def add_residual(chunk, c, b):
                dve.wait_ge(out_done, chunk + 1)
                dve.wait_ge(xres_ready, chunk + 1)
                dve.tensor_tensor(xres[:, c], ring[b][:], xres[:, c], ALU.add).then_inc(x1_ready, 1)

            def f_stats_of(b, loads, parity):
                dve.wait_ge(x1_loaded[parity], 16 * loads)
                for t in range(NT):
                    dve.bn_stats(bn[:, t], x1b[parity][:, t]).then_inc(f_bn, 1)
                dve.wait_ge(f_bn, NT * b + NT)
                dve.memset(wait_pad[:], 0.0)
                for t in range(NT):
                    dve.bn_aggr(mean_var[:, t], bn[:, t]).then_inc(f_stats, 1)

            def f_normalise(b, parity):
                dve.wait_ge(f_rstd, b + 1)
                if isinstance(b, int) and b == 0:
                    dve.wait_ge(v_done, 2 * NB)
                else:
                    dve.wait_ge(f_turned, KC * b)
                for t in range(NT):
                    dve.tensor_scalar(x1n[:, t], x1b[parity][:, t], mean_var[:, t, 0:1], rstd[:, t:t + 1],
                                      ALU.subtract, ALU.mult).then_inc(f_norm, 1)

            steps = [0]

            def link(ins):
                steps[0] += 1
                ins.then_inc(setup_step, 1)
                dve.wait_ge(setup_step, steps[0])

            link(dve.memset(head_mask[:], 0.0))
            for j in range(HG):
                last = dve.memset(head_mask[HD * j:HD * j + HD, HV * j:HV * j + HV], 1.0)
            link(last)
            dve.wait_ge(biases_loaded, 48)
            dve.tensor_scalar(neg_bqk_cols[:], bqk_cols[:], -1.0, None, ALU.mult).then_inc(neg_ready, 1)
            normalise(0, 1, 0)
            dve.wait_ge(silu_ready, 1)
            dve.wait_ge(consts_ready, 2)
            for k in range(KC):
                last = dve.tensor_scalar(silu_wide[:, k], ones_row[:], silu_c[:, k:k + 1], None, ALU.mult)
            last.then_inc(wide_ready, 1)
            normalise2(0, 0)
            dve.wait_ge(cols_done, 1)
            dve.tensor_copy(mod_cols[:, 0:KC], ring[1][:, 0:KC])
            dve.tensor_scalar(mod_cols[:, KC:2 * KC], ring[1][:, KC:2 * KC], 1.0, None, ALU.add).then_inc(cols_ready, 1)
            dve.wait_ge(wqkv_loaded, 16)
            link(dve.tensor_copy(wqkv_h[:], stage_w[:]))
            dve.tensor_tensor(wqkv_l[:], stage_w[:], wqkv_h[:].bitcast(F32), ALU.subtract).then_inc(wqkv_ready, 1)
            dve.wait_ge(wqkv_ready, 1)
            dve.sem_inc(stage_free, 1)
            split_h(0)
            normalise(1, 1, 1)
            normalise2(1, 1)
            dve.wait_ge(biases_loaded, 48)
            for g in range(4):
                elu_sum(0, g, 0)
            values(0, 0, 0, 0)
            values(0, 1, 0, 1)
            split_h(1)

            def gate_rows(src):
                link(dve.tensor_scalar(sgn_rows, src, 0.0, 2.0, ALU.is_ge, ALU.mult))
                link(dve.tensor_scalar(sgn_rows, sgn_rows, -1.0, None, ALU.add))
                link(dve.tensor_scalar(abs_rows, src, -1.0, 0.25, ALU.mult, ALU.max))
                link(dve.tensor_tensor(abs_rows, src, abs_rows, ALU.max))

            dve.wait_ge(rows_done, 1)
            dve.memset(qpad_h[:].bitcast(F32), 0.0)
            dve.memset(qpad_l[:].bitcast(F32), 0.0).then_inc(pads_cleared, 1)
            gate_rows(bank[0][:])
            link(dve.tensor_tensor(ga_rows, sgn_rows, abs_rows, ALU.mult))
            link(dve.tensor_tensor(gab_rows[:], gab_rows[:], ga_rows, ALU.mult))
            dve.wait_ge(wout_loaded, 16)
            link(dve.tensor_tensor(stage_w[:, :, 0:C], stage_w[:, :, 0:C],
                                   ga_rows.unsqueeze(1).broadcast_to((P, KC, C)), ALU.mult))
            link(dve.tensor_copy(wout_h[:], stage_w[:, :, 0:C]))
            dve.tensor_tensor(wout_l[:], stage_w[:, :, 0:C], wout_h[:].bitcast(F32), ALU.subtract)\
               .then_inc(wout_ready, 1)
            gate_rows(bank[1][:])
            link(dve.tensor_tensor(gb_rows[:], sgn_rows, abs_rows, ALU.mult))
            link(dve.tensor_scalar(gb_rows[:], gb_rows[:], W_SCALE, W_SCALE, ALU.mult, ALU.mult))
            dve.tensor_copy(mod_cols[:, 2 * KC:3 * KC], bank[2][:, 0:KC])
            dve.tensor_scalar(mod_cols[:, 3 * KC:4 * KC], bank[2][:, KC:2 * KC], 1.0, None, ALU.add)
            dve.wait_ge(state_zeroed, 1)
            dve.wait_ge(wout_ready, 1)
            mask_state()
            dve.wait_ge(state_ready, 1)
            dve.sem_inc(rows_ready, 1)
            spread_low(0, 0, 0)

            def step(i, half, parity, first, has_x, has_proj):
                other = 1 - parity
                mask_scores(2 * i)
                if not first:
                    ctx_low(2 * i - 1, 1, 0)
                if has_proj:
                    elu_sum(i + 1, 0, other)
                spread_low(2 * i + 1, parity, 1)
                if has_proj:
                    elu_sum(i + 1, 1, other)
                if has_x:
                    normalise(i + 2, half + 2, parity)
                if not has_proj:
                    f_stats_of(0, 1, 0)
                if has_proj:
                    elu_sum(i + 1, 2, other)
                context(2 * i)
                if has_proj:
                    elu_sum(i + 1, 3, other)
                dve.wait_ge(state_done, 2 * i + 1)
                mask_state()
                if not first:
                    add_residual(2 * i - 1, 1, 1)
                mask_scores(2 * i + 1)
                if has_proj:
                    values(i + 1, 0, other, 1)
                    values(i + 1, 1, other, 0)
                ctx_low(2 * i, 0, 1)
                if has_proj:
                    spread_low(2 * i + 2, other, 0)
                if has_x:
                    normalise2(i + 2, parity)
                add_residual(2 * i, 0, 1)
                context(2 * i + 1)
                if not has_proj:
                    f_normalise(0, 0)
                dve.wait_ge(state_done, 2 * i + 2)
                mask_state()
                if has_x:
                    split_h(i + 2)

            phase1_blocks(dve, step)
            ctx_low(2 * NB - 1, 1, 0)
            add_residual(2 * NB - 1, 1, 1)

            def f_split(b, parity, pair):
                high, low = g_hl[parity]
                if not (isinstance(b, int) and b < 2):
                    dve.wait_ge(gu_done, KF * (b - 1))
                for k in (2 * pair, 2 * pair + 1):
                    dve.wait_ge(f_mod, KC * b + k + 1)
                    dve.tensor_copy(high[:, k], gf[:, k % 2]).then_inc(f_h, 1)
                    dve.wait_ge(f_h, KC * b + k + 1)
                    dve.tensor_tensor(low[:, k], gf[:, k % 2], high[:, k].bitcast(F32), ALU.subtract)\
                       .then_inc(f_l, 1)

            def hidden(b, k):
                dve.wait_ge(sil_ready, KF * b + k + 1)
                if not (isinstance(b, int) and b == 0 and k < 2):
                    dve.wait_ge(hid_l_ready, KF * b + k - 1)
                dve.tensor_tensor(hid[:, k % 2], bank[5 + 2 * (k % 2)][:], sil[:, k % 2], ALU.mult)\
                   .then_inc(hid_ready, 1)

            def hid_low(b, k):
                dve.wait_ge(hid_h_ready, KF * b + k + 1)
                dve.tensor_tensor(hid_l[:, k % 4], hid[:, k % 2], hid_h[:, k % 4].bitcast(F32), ALU.subtract)\
                   .then_inc(hid_l_ready, 1)

            def scale_down(b):
                dve.wait_ge(down_k, KF * b + KF)
                if not (isinstance(b, int) and b == 0):
                    dve.wait_ge(y_stored, 16 * b)
                for t in range(NT):
                    dve.tensor_tensor(y[:, t], bank[t][:], gb_rows[:], ALU.mult).then_inc(scaled, 1)

            def add_x1(b, parity):
                for t in range(NT):
                    dve.wait_ge(scaled, NT * b + t + 1)
                    dve.tensor_tensor(y[:, t], y[:, t], x1b[parity][:, t], ALU.add).then_inc(y_ready, 1)

            f_split(0, 0, 0)
            f_split(0, 0, 1)

            def fstep(b, half, parity, first, has_next):
                other = 1 - parity
                hidden(b, 0)
                for k in range(KF):
                    if k == TURN_AT and has_next:
                        f_split(b + 1, other, 0)
                        f_split(b + 1, other, 1)
                    if k + 1 < KF:
                        hidden(b, k + 1)
                    hid_low(b, k)
                    if k == 0 and not first:
                        scale_down(b - 1)
                    if k == 1 and not first:
                        add_x1(b - 1, other)
                    if k == TURN_AT - 3 and has_next:
                        f_stats_of(b + 1, half + parity + 1, other)
                    if k == TURN_AT - 2 and has_next:
                        f_normalise(b + 1, other)

            phase2_blocks(dve, fstep)
            scale_down(NF - 1)
            add_x1(NF - 1, 1)

        @block.tensor
        def _(pe):
            def mod_columns(out_bank, wm):
                for s in range(2):
                    for m in range(KC):
                        for k in range(KC):
                            last = pe.matmul(out_bank[:, s * KC + m:s * KC + m + 1],
                                             wm[:, k, s * C + m * P:s * C + (m + 1) * P], silu_c[:, k:k + 1],
                                             start=(k == 0), stop=(k == KC - 1))
                return last

            def mod_rows(out_bank, wm):
                for k in range(KC):
                    last = pe.matmul(out_bank[:, 0:C], silu_wide[:, k], wm[:, k], start=(k == 0), stop=(k == KC - 1))
                return last

            def turn_x(m, u):
                for q in range(2):
                    for t in range(2):
                        k = 2 * u + q
                        last = pe.transpose(ring[u][:, q * TB + t * P:q * TB + (t + 1) * P],
                                            xn[:, t, k * P:(k + 1) * P], ident[:])
                last.then_inc(x_turned, 1)

            hs = (hh, hl, hh)
            ws = (wqkv_h, wqkv_h, wqkv_l)

            def qk_matmul(g, d, b):
                s, r = d // 12, d % 12
                k, q = r // 3, r % 3
                last = pe.matmul(ring[b][:, s * TB:(s + 1) * TB], ws[q][:, k, s * C + g * P:s * C + (g + 1) * P],
                                 hs[q][:, k], start=(r == 0), stop=(r == 11))
                if d == 23:
                    last.then_inc(qk_done, 1)

            def v_matmul(c, d, b):
                k, q = d // 3, d % 3
                last = pe.matmul(ring[b][:, :], hs[q][:, k, c * CH:(c + 1) * CH], ws[q][:, k, 2 * C:3 * C],
                                 start=(d == 0), stop=(d == 11))
                if d == 11:
                    last.then_inc(v_done, 1)

            def turn_k(n, u, b, parity):
                pe.wait_ge(qk_ready, 4 * n + 2 * u + 2)
                for q in range(2):
                    for c in range(2):
                        last = pe.transpose(ring[b][:, (2 * q + c) * P:(2 * q + c + 1) * P],
                                            qk[:, parity, 2 * u + q, 1, c * CH:(c + 1) * CH], ident[:])
                last.then_inc(k_turned, 1)

            def scores(chunk):
                pe.wait_ge(pad_l_ready, chunk + 1)
                if not (isinstance(chunk, int) and chunk == 0):
                    pe.wait_ge(ctx_ready, chunk)
                for g in range(KC):
                    for q in range(3):
                        last = pe.matmul(bank[g][:], (k_h, k_h, k_l)[q][:, g],
                                         (qpad_h, qpad_l, qpad_h)[q][:, g].rearrange("p j t -> p (j t)"),
                                         start=(q == 0), stop=(q == 2))
                    last.then_inc(scores_done, 1)

            def from_state(chunk, parity, c):
                pe.wait_ge(masked_ready, 4 * chunk + 2)
                pe.wait_ge(state_ready, chunk + 1)
                for g in range(KC):
                    pe.matmul(bank[g // 2][:, (g % 2) * GV:(g % 2 + 1) * GV], qk[:, parity, g, 0, c * CH:(c + 1) * CH],
                              state[:, g], start=(g % 2 == 0), stop=False, skip_group_check=True)

            def context_matmul(chunk, parity, c, n):
                g, j = n // HG, n % HG
                if j == 0:
                    pe.wait_ge(masked_ready, 4 * chunk + g + 1)
                u = n // (H // 2)
                at_col = (n % (H // 2)) * HV
                last = pe.matmul(bank[u][:, at_col:at_col + HV], masked[:, g, j], v_rows[:, parity, c, n * HV:(n + 1) * HV],
                                 start=False, stop=(n % (H // 2) == H // 2 - 1), skip_group_check=True)
                if n == H - 1:
                    last.then_inc(context_done, 1)

            def add_to_state(parity, c):
                for g in range(KC):
                    last = pe.matmul(state_bank[g // 2][:, (g % 2) * GV:(g % 2 + 1) * GV], k_rows[:, parity, c, g],
                                     v_rows[:, parity, c, g * GV:(g + 1) * GV], start=False, stop=True,
                                     skip_group_check=True)
                last.then_inc(state_done, 1)

            def turn_ctx(chunk, b):
                pe.wait_ge(ctx_ready, chunk + 1)
                for k in range(KC):
                    last = pe.transpose(ring[b][:, k * P:(k + 1) * P], ctx_rows[:, k * P:(k + 1) * P], ident[:])
                last.then_inc(ctx_turned, 1)

            def out_matmul(c, d, b):
                k, q = d // 3, d % 3
                last = pe.matmul(ring[b][:, :], (ctx_h, ctx_l, ctx_h)[q][:, c, k], (wout_h, wout_h, wout_l)[q][:, k],
                                 start=(d == 0), stop=(d == 11))
                if d == 11:
                    last.then_inc(out_done, 1)

            pe.wait_ge(silu_ready, 1)
            pe.wait_ge(mod1_loaded, 16)
            mod_columns(ring[1], stage_m).then_inc(cols_done, 1)
            pe.wait_ge(consts_ready, 2)
            pe.wait_ge(xn_ready, 2)
            turn_x(0, 0)
            pe.wait_ge(cols_ready, 1)
            turn_x(0, 1)
            pe.wait_ge(wqkv_ready, 1)
            pe.wait_ge(hl_ready, 2)
            pe.wait_ge(hf_ready, 4)
            for g in range(4):
                if g >= 2:
                    pe.wait_ge(qk_read, g - 1)
                for d in range(24):
                    qk_matmul(g, d, g % 2)
            pe.wait_ge(qk_read, 3)
            turn_k(0, 0, 0, 0)
            pe.wait_ge(qk_read, 4)
            turn_k(0, 1, 1, 0)
            for c in range(2):
                pe.wait_ge(k_rows_ready, c + 1)
                for d in range(12):
                    v_matmul(c, d, c)
            pe.wait_ge(xn_ready, 4)
            for u in range(2):
                pe.wait_ge(v_ready, u + 1)
                turn_x(1, u)
            pe.wait_ge(wide_ready, 1)
            pe.wait_ge(mod_ga_loaded, 16)
            pe.wait_ge(mod_gb_loaded, 16)
            pe.wait_ge(mod2_loaded, 16)
            mod_rows(bank[0], stage_w[:, :, C:2 * C])
            mod_rows(bank[1], stage_w[:, :, 2 * C:3 * C])
            mod_columns(bank[2], stage_m).then_inc(rows_done, 1)
            for u in range(2):
                last = pe.matmul(state_bank[u][:, 0:2 * GV], masked[:, 0, 0], masked[:, 0].rearrange("p j t -> p (j t)")[:, 0:2 * GV],
                                 start=True, stop=True)
            last.then_inc(state_zeroed, 1)
            pe.wait_ge(rows_ready, 1)

            def step(i, half, parity, first, has_x, has_proj):
                n, other = i + 1, 1 - parity
                scores(2 * i)
                if not first:
                    if has_proj:
                        pe.wait_ge(hf_ready, 4 * n + 2)
                    else:
                        pe.wait_ge(k_rows_ready, 2 * i + 2)
                    turn_ctx(2 * i - 1, 0)
                if has_proj:
                    pe.wait_ge(hl_ready, 2 * n + 2)
                    for d in range(24):
                        qk_matmul(0, d, 1)
                    if not first:
                        pe.wait_ge(ctx_l_ready, 2 * i)
                    for d in range(24):
                        qk_matmul(1, d, 0)
                from_state(2 * i, parity, 0)
                if has_proj:
                    pe.wait_ge(qk_read, 4 * n + 1)
                pe.wait_ge(v_ready, 2 * i + 1)
                for h in range(H):
                    context_matmul(2 * i, parity, 0, h)
                    if has_proj:
                        for d in range(h * 24 // H, (h + 1) * 24 // H):
                            qk_matmul(2, d, 1)
                if has_proj:
                    pe.wait_ge(qk_read, 4 * n + 2)
                    for d in range(24):
                        qk_matmul(3, d, 0)
                pe.wait_ge(k_rows_ready, 2 * i + 2)
                add_to_state(parity, 0)
                if not first:
                    pe.wait_ge(ctx_l_ready, 2 * i)
                    if has_proj:
                        pe.wait_ge(qk_read, 4 * n + 3)
                    else:
                        pe.wait_ge(x1_ready, 2 * i - 1)
                    for d in range(12):
                        out_matmul(1, d, 1)
                if has_proj:
                    pe.wait_ge(qk_read, 4 * n + 4)
                    turn_k(n, 0, 0, other)
                scores(2 * i + 1)
                if has_proj:
                    if first:
                        pe.wait_ge(qk_read, 4 * n + 3)
                    else:
                        pe.wait_ge(x1_ready, 2 * i)
                    for d in range(12):
                        v_matmul(0, d, 1)
                    pe.wait_ge(k_rows_ready, 2 * n + 1)
                    for d in range(12):
                        v_matmul(1, d, 0)
                    pe.wait_ge(v_ready, 2 * n + 1)
                elif not first:
                    pe.wait_ge(x1_ready, 2 * i)
                turn_ctx(2 * i, 1)
                if has_proj:
                    pe.wait_ge(v_ready, 2 * n + 2)
                    turn_k(n, 1, 0, other)
                from_state(2 * i + 1, parity, 1)
                pe.wait_ge(v_ready, 2 * i + 2)
                pe.wait_ge(ctx_l_ready, 2 * i + 1)
                for h in range(H):
                    context_matmul(2 * i + 1, parity, 1, h)
                    for d in range(h * 12 // H, (h + 1) * 12 // H):
                        out_matmul(0, d, 1)
                add_to_state(parity, 1)
                if has_x:
                    pe.wait_ge(xn_ready, 2 * i + 6)
                    pe.wait_ge(k_rows_ready, 2 * n + 2)
                    turn_x(i + 2, 0)
                    pe.wait_ge(x1_ready, 2 * i + 1)
                    turn_x(i + 2, 1)

            pe.wait_ge(wout_ready, 1)
            phase1_blocks(pe, step)
            turn_ctx(2 * NB - 1, 0)
            pe.wait_ge(ctx_l_ready, 2 * NB)
            pe.wait_ge(x1_ready, 2 * NB - 1)
            for d in range(12):
                out_matmul(1, d, 1)

            def f_turn(b, pair):
                for k in (2 * pair, 2 * pair + 1):
                    for t in range(NT):
                        last = pe.transpose(bank[turn_bank[k]][:, t * P:(t + 1) * P], x1n[:, t, k * P:(k + 1) * P],
                                            ident[:])
                    last.then_inc(f_turned, 1)

            def gate_up(b, kf, parity):
                for s, w in ((0, wg), (1, wu)):
                    for k in range(KC):
                        for half in range(2):
                            last = pe.matmul(bank[4 + 2 * (kf % 2) + s][:], w[:, k, kf * P:(kf + 1) * P],
                                             g_hl[parity][half][:, k], start=(k == 0 and half == 0),
                                             stop=(k == KC - 1 and half == 1))
                last.then_inc(gu_done, 1)

            def down(b, kf):
                pe.wait_ge(hid_l_ready, KF * b + kf + 1)
                for t in range(NT):
                    for half, hid_x in ((0, hid_h), (1, hid_l)):
                        last = pe.matmul(bank[t][:], hid_x[:, kf % 4, t * P:(t + 1) * P], wd[:, kf],
                                         start=(kf == 0 and half == 0), stop=(kf == KF - 1 and half == 1))
                last.then_inc(down_k, 1)

            pe.wait_ge(f_norm, NT)
            pe.wait_ge(x1_ready, 2 * NB)
            pe.wait_ge(state_ready, 2 * NB + 1)
            f_turn(0, 0)
            f_turn(0, 1)
            pe.wait_ge(wg_loaded, 16)
            pe.wait_ge(wu_loaded, 16)

            def fstep(b, half, parity, first, has_next):
                pe.wait_ge(f_l, KC * b + KC)
                for kf in range(KF):
                    if kf == TURN_AT + 1 and has_next:
                        pe.wait_ge(f_norm, NT * b + 2 * NT)
                        pe.wait_ge(hid_ready, KF * b + kf - 1)
                        f_turn(b + 1, 0)
                        down(b, kf - 2)
                        pe.wait_ge(hid_ready, KF * b + kf)
                        f_turn(b + 1, 1)
                        pe.wait_ge(f_mod, KC * b + KC + 2)
                    elif kf == TURN_AT + 2 and has_next:
                        pe.wait_ge(f_mod, KC * b + KC + 4)
                    elif not (first and kf < 2):
                        pe.wait_ge(hid_ready, KF * b + kf - 1)
                    gate_up(b, kf, parity)
                    if kf == 0 and not first:
                        down(b - 1, KF - 1)
                    if kf == 2:
                        if first:
                            pe.wait_ge(wd_loaded, 16)
                        else:
                            pe.wait_ge(scaled, NT * b)
                    if kf >= 2 and not (kf == TURN_AT + 1 and has_next):
                        down(b, kf - 2)
                down(b, KF - 2)

            phase2_blocks(pe, fstep)
            down(NF - 1, KF - 1)


_IN_ORDER = ("x", "wqkv_t", "b_qk", "b_v", "wout_t", "b_out", "wg_t", "wu_t", "wd_t", "c_in", "wmod")


def kernel(**inputs):
    import numpy as _np
    import concourse.bacc as _bacc
    from concourse import mybir as _mybir
    from concourse.bass_utils import run_bass_kernel_spmd as _run

    nc = _bacc.Bacc("TRN2", target_bir_lowering=False, num_devices=1)
    x = _np.asarray(inputs["L0_attn_x"])
    C = x.shape[2]
    b_qkv = _np.asarray(inputs["L0_attn_b_qkv"])
    laid = {
        "x": x.reshape(x.shape[1], x.shape[2]),
        "wqkv_t": _np.asarray(inputs["L0_attn_w_qkv"]).T,
        "b_qk": b_qkv[:2 * C].reshape(2 * C // P, P).T,
        "b_v": b_qkv[2 * C:],
        "wout_t": _np.asarray(inputs["L0_attn_w_out"]).T,
        "b_out": _np.asarray(inputs["L0_attn_b_out"]),
        "wg_t": _np.asarray(inputs["L0_ffn_w_gate"]).T,
        "wu_t": _np.asarray(inputs["L0_ffn_w_up"]).T,
        "wd_t": _np.asarray(inputs["L0_ffn_w_down"]).T,
        "c_in": _np.asarray(inputs["L0_c"]).reshape(C // P, P).T,
        "wmod": _np.asarray(inputs["L0_wmod"]),
    }
    arrays, args = {}, []
    for name in _IN_ORDER:
        a = _np.ascontiguousarray(laid[name])
        arrays[f"in_{name}"] = a
        args.append(nc.dram_tensor(f"in_{name}", a.shape, _mybir.dt.from_np(a.dtype), kind="ExternalInput").ap())
    out = nc.dram_tensor("out_x", laid["x"].shape, _mybir.dt.float32, kind="ExternalOutput").ap()
    adaln_block(nc, *args, out)
    r = _run(nc, [arrays], core_ids=[0])
    return r.results[0]["out_x"].reshape(x.shape)
```

```python
from contextlib import ExitStack

import concourse.bass as bass
from concourse import mybir

F32 = mybir.dt.float32
F32R = mybir.dt.float32r
I32 = mybir.dt.int32
ALU = mybir.AluOpType
ACT = mybir.ActivationFunctionType

P = 128
HD = 32
HG = P // HD
HV = HD + 1
LN_EPS = 1e-5
ATTN_EPS = 1e-6
W_SCALE = 1.0 / 127.0
W_HELD = 4096.0
AX = mybir.AxisListType.X


def adaln_block(nc, x, wqkv_t, b_qk, b_v, wout_t, b_out, w_ffn, c_in, wmod_t, out):
    T, C = x.shape
    F = w_ffn.shape[0] // 3 // C
    wg_t, wu_t = (w_ffn[i * C * F:(i + 1) * C * F].rearrange("(k p n) -> p k n", p=P, n=F) for i in (0, 1))
    wd_t = w_ffn[2 * C * F:3 * C * F].rearrange("(k p n) -> p k n", p=P, n=C)
    KC = C // P
    KF = F // P
    H = C // HD
    GV = HG * HV
    CH = P
    TB = 2 * CH
    NB = T // TB
    NT = 4
    FB = NT * P
    NF = T // FB
    assert NB % 2 == 0 and NB >= 6 and NF % 2 == 0 and KC == 4 and KF % 2 == 0

    MID = 1
    SCORE_ORDER = (2, 3, 0, 1)
    TURN_AT = KF - 4
    turn_bank = (6, 7, 4, 5)
    NP = 3 * C * F // (NB * P)
    w_pieces = w_ffn.rearrange("(n p c) -> n p c", p=P, c=NP)
    x_blocks = x.rearrange("(n t p) c -> n p t c", p=P, t=2)
    x_chunks = x.rearrange("(n p) c -> n p c", p=P)
    x1_dram = nc.dram_tensor("x1_dram", (T, C), F32, kind="Internal").ap()
    x1_chunks = x1_dram.rearrange("(n p) c -> n p c", p=P)
    x1_blocks = x1_dram.rearrange("(n t p) c -> n p t c", p=P, t=NT)
    gates_dram = nc.dram_tensor("gates_dram", (2, C), F32, kind="Internal").ap()
    out_blocks = out.rearrange("(n t p) c -> n p t c", p=P, t=NT)

    with ExitStack() as ctx:
        def sem(name):
            return ctx.enter_context(nc.semaphore(name))

        base = (nc.sbuf_base + 63) // 64 * 64
        top = [base]

        def at(name, shape, dtype, offset):
            return nc.alloc_sbuf_tensor_at(name, shape, dtype, offset=offset)

        def sb(name, shape, dtype):
            n = 4
            for s in shape[1:]:
                n *= s
            t = at(name, shape, dtype, top[0])
            top[0] += (n + 31) // 32 * 32
            return t

        ident = sb("ident", (P, P), F32)
        mod_cols = sb("mod_cols", (P, 4 * KC), F32)
        gb_rows = sb("gb_rows", (P, C), F32)
        neg_half = sb("neg_half", (P, NT), F32)
        eps_cols = sb("eps_cols", (P, NT), F32)
        wait_pad = sb("wait_pad", (P, 1), F32)
        mean_var = sb("mean_var", (P, NT, 2), F32)
        var_eps = sb("var_eps", (P, NT), F32)
        rstd = sb("rstd", (P, NT), F32)
        bn = sb("bn", (P, NT, 6), F32)
        wqkv_at = top[0]
        wqkv_h = sb("wqkv_h", (P, KC, 3 * C), F32R)
        wqkv_l = sb("wqkv_l", (P, KC, 3 * C), F32R)
        wu = at("wu", (P, KC, F), F32R, wqkv_at)
        wd = at("wd", (P, KF, C), F32R, wqkv_at + KC * F * 4)
        wout_h = sb("wout_h", (P, KC, C), F32R)
        wout_l = sb("wout_l", (P, KC, C), F32R)
        wu_full = at("wu_full", (P, KC, F), F32, wqkv_at)
        wd_full = at("wd_full", (P, KF, C), F32, wqkv_at + KC * F * 4)
        stage_at = top[0]
        stage_w = sb("stage_w", (P, KC, 3 * C), F32)
        stage_m = sb("stage_m", (P, 2, KC, C), F32)
        stage_m2 = at("stage_m2", (P, 3, KC, C), F32, stage_at)
        wg = at("wg", (P, KC, F), F32R, stage_at)
        wg_full = at("wg_full", (P, KC, F), F32, stage_at)
        qpad_h = at("qpad_h", (P, KC, HG, CH), F32R, stage_at + KC * F * 4)
        qpad_l = at("qpad_l", (P, KC, HG, CH), F32R, stage_at + (KC * F + KC * HG * CH) * 4)
        assert KC * F == KC * 3 * C and HG * CH == C
        phase1_at = top[0]
        xb = sb("xb", (P, 2, 2, C), F32)
        xn = sb("xn", (P, 2, C), F32)
        hf = sb("hf", (P, KC, TB), F32)
        hh = sb("hh", (P, KC, TB), F32R)
        hl = sb("hl", (P, KC, TB), F32R)
        e_part = sb("e_part", (P, 2, 2, TB), F32)
        r_part = sb("r_part", (P, 2, 2, TB), F32)
        early_end = top[0]
        qk = sb("qk", (P, 2, KC, 2, TB), F32)
        k_rows = sb("k_rows", (P, 2, 2, KC, P), F32)
        v_rows = sb("v_rows", (P, 2, 2, H * HV), F32)
        k_h = sb("k_h", (P, KC, CH), F32R)
        k_l = sb("k_l", (P, KC, CH), F32R)
        masked = sb("masked", (P, KC, HG, CH), F32)
        state = sb("state", (P, KC, GV), F32)
        ctx_rows = sb("ctx_rows", (P, C), F32)
        den = sb("den", (P, H), F32)
        rden = sb("rden", (P, H), F32)
        ctx_h_at = top[0]
        ctx_h = sb("ctx_h", (P, 2, KC, CH), F32R)
        ctx_l_at = top[0]
        ctx_l = sb("ctx_l", (P, 2, KC, CH), F32R)
        silu_rows = at("silu_rows", (P, C), F32, ctx_h_at + C * 4)
        products = at("products", (P, C), F32, ctx_l_at + C * 4)
        xres = sb("xres", (P, 2, C), F32)
        causal = sb("causal", (P, CH), F32)
        head_mask = sb("head_mask", (P, GV), F32)
        bqk_cols = sb("bqk_cols", (P, 2 * KC), F32)
        neg_bqk_cols = sb("neg_bqk_cols", (P, 2 * KC), F32)
        bv_rows = sb("bv_rows", (P, C), F32)
        gab_rows = sb("gab_rows", (P, C), F32)
        gates = sb("gates", (P, 4, KC), F32)
        ones_row = sb("ones_row", (P, P), F32)
        piece_at = top[0]
        piece = sb("piece", (P, NP), I32)
        assert NP >= FB
        gf_first = at("gf_first", (P, FB), F32, piece_at)
        piece_ends = sb("piece_ends", (P, 2), F32)
        w_ends = sb("w_ends", (P, 2), F32)
        w_held = sb("w_held", (P, 3), F32)
        count = sb("count", (P, 1), I32)
        ga_rows = masked[:, 1].rearrange("p g t -> p (g t)")
        assert top[0] <= nc.sbuf_usable_end
        top[0] = phase1_at
        x1b = [sb("x1b0", (P, NT, C), F32), None]
        x1n = sb("x1n", (P, NT, C), F32)
        g_hl = [[None, None], [None, None]]
        g_hl[0][0] = sb("g_h0", (P, KC, FB), F32R)
        g_hl[0][1] = sb("g_l0", (P, KC, FB), F32R)
        assert top[0] <= early_end
        x1b[1] = sb("x1b1", (P, NT, C), F32)
        g_hl[1][0] = sb("g_h1", (P, KC, FB), F32R)
        g_hl[1][1] = sb("g_l1", (P, KC, FB), F32R)
        gf = sb("gf", (P, 2, FB), F32)
        sil = sb("sil", (P, 2, FB), F32)
        hid = sb("hid", (P, 2, FB), F32)
        hid_h = sb("hid_h", (P, 4, FB), F32R)
        hid_l = sb("hid_l", (P, 4, FB), F32R)
        y = sb("y", (P, NT, C), F32)
        assert top[0] <= nc.sbuf_usable_end

        bank = [ctx.enter_context(nc.psum_tensor(f"bank{b}", (P, 512), F32)) for b in range(8)]
        state_bank = bank[4:6]
        ring = bank[6:8]

        consts_ready = sem("consts_ready")
        c_loaded = sem("c_loaded")
        bias_cols_loaded = sem("bias_cols_loaded")
        bias_rows_loaded = sem("bias_rows_loaded")
        silu_ready = sem("silu_ready")
        wmod_loaded = [sem(f"wmod_loaded{s}") for s in range(6)]
        cols_ready = sem("cols_ready")
        wqkv_loaded = [sem(f"wqkv_loaded{k}") for k in range(KC + 1)]
        wqkv_h_ready = sem("wqkv_h_ready")
        wqkv_ready = sem("wqkv_ready")
        wqkv_mid_ready = sem("wqkv_mid_ready")
        wmod_scaled = sem("wmod_scaled")
        wmod_summed = sem("wmod_summed")
        neg_ready = sem("neg_ready")
        gab_ready = sem("gab_ready")
        gates_ready = sem("gates_ready")
        gates_stored = sem("gates_stored")
        gates_loaded = sem("gates_loaded")
        wout_loaded = sem("wout_loaded")
        wout_scaled = sem("wout_scaled")
        wout_h_ready = sem("wout_h_ready")
        wout_ready = sem("wout_ready")
        state_zeroed = sem("state_zeroed")
        setup_step = sem("setup_step")
        wg_loaded = sem("wg_loaded")
        wu_loaded = sem("wu_loaded")
        wd_loaded = sem("wd_loaded")

        x_loaded = [sem("x_loaded0"), sem("x_loaded1")]
        bn_done = sem("bn_done")
        stats_ready = sem("stats_ready")
        var_ready = sem("var_ready")
        rstd_ready = sem("rstd_ready")
        xn_ready = sem("xn_ready")
        x_turned = sem("x_turned")
        hf_ready = sem("hf_ready")
        hh_ready = sem("hh_ready")
        hl_ready = sem("hl_ready")
        qk_done = sem("qk_done")
        qk_read = sem("qk_read")
        elu_parts = sem("elu_parts")
        qk_ready = sem("qk_ready")
        k_turned = sem("k_turned")
        k_rows_ready = sem("k_rows_ready")
        v_done = sem("v_done")
        v_ready = sem("v_ready")
        pad_h_cleared = sem("pad_h_cleared")
        pad_l_cleared = sem("pad_l_cleared")
        pad_h_ready = sem("pad_h_ready")
        pad_l_ready = sem("pad_l_ready")
        scores_done = sem("scores_done")
        masked_ready = sem("masked_ready")
        context_done = sem("context_done")
        den_ready = sem("den_ready")
        rden_ready = sem("rden_ready")
        ctx_ready = sem("ctx_ready")
        state_done = sem("state_done")
        state_ready = sem("state_ready")
        ctx_turned = sem("ctx_turned")
        ctx_h_ready = sem("ctx_h_ready")
        ctx_l_ready = sem("ctx_l_ready")
        out_done = sem("out_done")
        xres_loaded = [sem("xres_loaded0"), sem("xres_loaded1")]
        xres_ready = sem("xres_ready")
        x1_ready = sem("x1_ready")
        x1_stored = [sem("x1_stored0"), sem("x1_stored1")]

        piece_loaded = sem("piece_loaded")
        piece_read = sem("piece_read")
        ends_ready = sem("ends_ready")
        bounds_ready = sem("bounds_ready")
        held_ready = sem("held_ready")
        count_done = sem("count_done")
        count_ready = sem("count_ready")
        full_loaded = sem("full_loaded")

        x1_loaded = [sem("x1_loaded0"), sem("x1_loaded1")]
        f_bn = sem("f_bn")
        f_stats = sem("f_stats")
        f_var = sem("f_var")
        f_rstd = sem("f_rstd")
        f_norm = sem("f_norm")
        f_turned = sem("f_turned")
        f_mod = sem("f_mod")
        f_h = sem("f_h")
        f_l = sem("f_l")
        gu_done = sem("gu_done")
        sil_ready = sem("sil_ready")
        hid_ready = sem("hid_ready")
        hid_h_ready = sem("hid_h_ready")
        hid_l_ready = sem("hid_l_ready")
        down_k = sem("down_k")
        scaled = sem("scaled")
        y_ready = sem("y_ready")
        last_down = sem("last_down")
        y_stored = sem("y_stored")

        block = ctx.enter_context(nc.Block())

        def phase1_blocks(eng, step):
            step(0, 0, 0, True, True, True)
            with eng.Fori(0, (NB - 4) // 2) as j:
                step(2 * j + 1, j, 1, False, True, True)
                step(2 * j + 2, j + 1, 0, False, True, True)
            step(NB - 3, (NB - 4) // 2, 1, False, True, True)
            step(NB - 2, (NB - 2) // 2, 0, False, False, True)
            step(NB - 1, (NB - 2) // 2, 1, False, False, False)

        def phase2_blocks(eng, step):
            step(0, 0, 0, True, True)
            with eng.Fori(0, (NF - 2) // 2) as j:
                step(2 * j + 1, j, 1, False, True)
                step(2 * j + 2, j + 1, 0, False, True)
            step(NF - 1, (NF - 2) // 2, 1, False, False)

        @block.sync
        def _(sp):
            def load_wmod(s, place, order):
                rows = wmod_t[s * C:(s + 1) * C].rearrange(order, p=P)
                sp.dma_start(place, rows).then_inc(wmod_loaded[s], 16)

            BY_TILE, BY_ROW = "(k p) c -> p k c", "(p k) c -> p k c"
            sp.dma_start(products[:], c_in.partition_broadcast(P)).then_inc(c_loaded, 16)
            sp.dma_start(xb[:, 0], x_blocks[0]).then_inc(x_loaded[0], 16)
            for s in range(2):
                load_wmod(s, stage_m[:, s], BY_TILE)
            for k in range(KC):
                sp.dma_start(stage_w[:, k, 0:2 * C], wqkv_t[k * P:(k + 1) * P, 0:2 * C]).then_inc(wqkv_loaded[k], 16)
                if k == 1:
                    sp.dma_start(bqk_cols[:], b_qk).then_inc(bias_cols_loaded, 16)
            sp.dma_start(xb[:, 1], x_blocks[1]).then_inc(x_loaded[1], 16)
            sp.dma_start(stage_w[:, :, 2 * C:3 * C], wqkv_t.rearrange("(k p) n -> p k n", p=P)[:, :, 2 * C:3 * C])\
              .then_inc(wqkv_loaded[KC], 16)
            sp.wait_ge(cols_ready, 1)
            load_wmod(2, stage_m[:, 0], BY_ROW)
            sp.dma_start(bv_rows[:], b_v.partition_broadcast(P)).then_inc(bias_rows_loaded, 16)
            sp.dma_start(gab_rows[:], b_out.partition_broadcast(P)).then_inc(bias_rows_loaded, 16)
            sp.wait_ge(wqkv_ready, KC)
            sp.wait_ge(wqkv_mid_ready, 1)
            sp.dma_start(stage_m2[:, 2], wout_t.rearrange("(k p) n -> p k n", p=P)).then_inc(wout_loaded, 16)
            for s in (3, 4):
                load_wmod(s, stage_m2[:, s - 3], BY_TILE)

            def spread_gate(i, rows):
                sp.wait_ge(gates_ready, i + 1)
                sp.dma_start(gates_dram[i].rearrange("(p k) -> p k", p=P), gates[:, i]).then_inc(gates_stored, 16)
                sp.wait_ge(gates_stored, 16 * (i + 1))
                sp.dma_start(rows, gates_dram[i].partition_broadcast(P)).then_inc(gates_loaded, 16)

            spread_gate(0, ga_rows)

            def store_x1(chunk, c):
                sp.wait_ge(x1_ready, chunk + 1)
                sp.dma_start(x1_chunks[chunk], xres[:, c]).then_inc(x1_stored[c], 16)

            def step(i, half, parity, first, has_x, has_proj):
                if not first:
                    sp.wait_ge(piece_read, 2 * i)
                sp.dma_start(piece[:], w_pieces[i]).then_inc(piece_loaded, 16)
                if has_x:
                    sp.wait_ge(xn_ready, 2 * i + 2)
                    sp.dma_start(xb[:, parity], x_blocks[i + 2]).then_inc(x_loaded[parity], 16)
                if has_proj and not has_x:
                    sp.wait_ge(xn_ready, 2 * NB)
                    sp.dma_start(x1b[0][:], x1_blocks[0]).then_inc(x1_loaded[0], 16)
                for c in range(2):
                    if not first:
                        sp.wait_ge(x1_stored[c], 16 * i)
                    sp.dma_start(xres[:, c], x_chunks[2 * i + c]).then_inc(xres_loaded[c], 16)
                    if first and c == 1:
                        sp.wait_ge(wout_ready, 1)
                        load_wmod(5, stage_m2[:, 2], BY_ROW)
                    if c == 1:
                        store_x1(2 * i, 0)
                    elif not first:
                        store_x1(2 * i - 1, 1)

            phase1_blocks(sp, step)
            spread_gate(1, gb_rows[:])
            store_x1(2 * NB - 1, 1)

            sp.wait_ge(x1_stored[0], 16 * NB)
            sp.wait_ge(x1_stored[1], 16 * NB)
            sp.dma_start(x1b[1][:], x1_blocks[1]).then_inc(x1_loaded[1], 16)

            def fstep(b, half, parity, first, has_next):
                sp.wait_ge(y_ready, NT * b + NT)
                sp.dma_start(out_blocks[b], y[:]).then_inc(y_stored, 16)

            def fstep_load(b, parity):
                sp.dma_start(x1b[parity][:], x1_blocks[b + 2]).then_inc(x1_loaded[parity], 16)

            fstep(0, 0, 0, True, True)
            fstep_load(0, 0)
            with sp.Fori(0, (NF - 4) // 2) as j:
                fstep(2 * j + 1, j, 1, False, True)
                fstep_load(2 * j + 1, 1)
                fstep(2 * j + 2, j + 1, 0, False, True)
                fstep_load(2 * j + 2, 0)
            fstep(NF - 3, None, 1, False, True)
            fstep_load(NF - 3, 1)
            fstep(NF - 2, None, 0, False, True)
            for pair in range(2):
                sp.wait_ge(y_ready, NT * (NF - 1) + 2 * pair + 2)
                sp.dma_start(out_blocks[NF - 1][:, 2 * pair:2 * pair + 2], y[:, 2 * pair:2 * pair + 2]).then_inc(y_stored, 16)
            sp.wait_ge(y_stored, 16 * (NF + 1))

        @block.gpsimd
        def _(pool):
            pool.memset(ident[:], 0.0)
            pool.memset(causal[:], 1.0)
            pool.memset(neg_half[:], -0.5)
            pool.memset(eps_cols[:], LN_EPS)
            pool.memset(ones_row[:], 1.0)
            pool.memset(v_rows[:], 1.0)
            pool.memset(masked[:, 0], 0.0).then_inc(consts_ready, 1)
            pool.wait_ge(consts_ready, 1)
            pool.affine_select(out=ident[:], in_=ident[:], compare_op=ALU.not_equal, fill=1.0, base=0,
                               pattern=[[-1, P]], channel_multiplier=1)
            pool.affine_select(out=causal[:], in_=causal[:], compare_op=ALU.is_ge, fill=0.0, base=0,
                               pattern=[[1, CH]], channel_multiplier=-1).then_inc(consts_ready, 1)

            def rstd_of(m):
                pool.wait_ge(stats_ready, 2 * m + 2)
                pool.tensor_tensor(var_eps[:, 0:2], mean_var[:, 0:2, 1], eps_cols[:, 0:2], ALU.add).then_inc(var_ready, 1)
                pool.wait_ge(var_ready, m + 1)
                pool.tensor_tensor(rstd[:, 0:2], var_eps[:, 0:2], neg_half[:, 0:2], ALU.pow).then_inc(rstd_ready, 1)

            def f_rstd_of(b):
                pool.wait_ge(f_stats, NT * b + NT)
                pool.tensor_tensor(var_eps[:], mean_var[:, :, 1], eps_cols[:], ALU.add).then_inc(f_var, 1)
                pool.wait_ge(f_var, b + 1)
                pool.tensor_tensor(rstd[:], var_eps[:], neg_half[:], ALU.pow).then_inc(f_rstd, 1)

            def residual(chunk, loads, c):
                pool.wait_ge(xres_loaded[c], 16 * loads)
                if isinstance(chunk, int) and chunk == 0:
                    pool.wait_ge(gab_ready, 1)
                pool.tensor_tensor(xres[:, c], xres[:, c], gab_rows[:], ALU.add).then_inc(xres_ready, 1)

            def scale_wmod(s):
                pool.wait_ge(wmod_loaded[s], 16)
                pool.tensor_tensor(stage_m2[:, s - 3], stage_m2[:, s - 3],
                                   silu_rows[:].unsqueeze(1).broadcast_to((P, KC, C)), ALU.mult).then_inc(wmod_scaled, 1)

            rstd_of(0)
            pool.wait_ge(wqkv_h_ready, MID + 1)
            pool.tensor_tensor(wqkv_l[:, MID, 0:2 * C], stage_w[:, MID, 0:2 * C],
                               wqkv_h[:, MID, 0:2 * C].bitcast(F32), ALU.subtract)\
                .then_inc(wqkv_mid_ready, 1)
            pool.wait_ge(cols_ready, 1)
            pool.memset(qpad_l[:].bitcast(F32), 0.0).then_inc(pad_l_cleared, 1)
            rstd_of(1)
            pool.wait_ge(silu_ready, 1)
            scale_wmod(3)
            scale_wmod(4)

            def step(i, half, parity, first, has_x, has_proj):
                residual(2 * i, i + 1, 0)
                if not has_proj:
                    pool.wait_ge(v_done, 2 * NB)
                    pool.wait_ge(piece_loaded, 16 * NB)
                    pool.dma_start(wu[:], wu_t).then_inc(wu_loaded, 16)
                    pool.dma_start(wd[:], wd_t).then_inc(wd_loaded, 16)
                if first:
                    scale_wmod(5)
                if has_x:
                    rstd_of(i + 2)
                elif has_proj:
                    f_rstd_of(0)
                residual(2 * i + 1, i + 1, 1)
                if first:
                    pool.wait_ge(wmod_summed, 3 * KC)
                    pool.dma_start(wg[:], wg_t).then_inc(wg_loaded, 16)

            phase1_blocks(pool, step)

            pool.wait_ge(count_ready, 1)
            held = pool.value_load(count[0:1, 0:1], min_val=0, max_val=P)
            with pool.If(held != P):
                for loaded in (wg_loaded, wu_loaded, wd_loaded):
                    pool.wait_ge(loaded, 16)
                pool.dma_start(wg_full[:], wg_t).then_inc(full_loaded, 16)
                pool.dma_start(wu_full[:], wu_t).then_inc(full_loaded, 16)
                pool.dma_start(wd_full[:], wd_t).then_inc(full_loaded, 16)
            with pool.Fori(1, NF) as b:
                f_rstd_of(b)

        @block.scalar
        def _(act):
            act.wait_ge(c_loaded, 16)
            act.activation(silu_rows[:], products[:], ACT.Silu).then_inc(silu_ready, 1)

            def turn_in(m, banks=ring):
                for u in range(2):
                    act.wait_ge(x_turned, 2 * m + u + 1)
                    if u == 0 and not (isinstance(m, int) and m == 0):
                        act.wait_ge(hl_ready, 2 * m)
                    for q in range(2):
                        k = 2 * u + q
                        act.activation(hf[:, k], banks[u][:, q * TB:(q + 1) * TB], ACT.Identity,
                                       bias=mod_cols[:, k:k + 1],
                                       scale=mod_cols[:, KC + k:KC + k + 1]).then_inc(hf_ready, 1)

            def elu(n, g, b):
                act.wait_ge(qk_done, 4 * n + g + 1)
                if g >= 2:
                    act.wait_ge(qk_ready, 4 * n + g - 1)
                for s in range(2):
                    act.activation(e_part[:, g % 2, s], ring[b][:, s * TB:(s + 1) * TB], ACT.Relu,
                                   bias=neg_bqk_cols[:, s * KC + g:s * KC + g + 1], scale=-1.0)
                for s in range(2):
                    last = act.activation(r_part[:, g % 2, s], ring[b][:, s * TB:(s + 1) * TB], ACT.Relu,
                                          bias=bqk_cols[:, s * KC + g:s * KC + g + 1])
                last.then_inc(qk_read, 1)
                act.wait_ge(qk_read, 4 * n + g + 1)
                act.activation(e_part[:, g % 2], e_part[:, g % 2], ACT.Exp, scale=-1.0).then_inc(elu_parts, 1)

            def k_in(n, u, from_bank, parity):
                act.wait_ge(k_turned, 2 * n + u + 1)
                act.activation(k_rows[:, parity, :, 2 * u:2 * u + 2, :],
                               from_bank[:, :].rearrange("p (g c d) -> p c g d", g=2, c=2), ACT.Copy)\
                   .then_inc(k_rows_ready, 1)

            def spread_high(chunk, parity, c):
                for j in range(HG):
                    rows = slice(HD * j, HD * (j + 1))
                    act.activation(qpad_h[rows, :, j], qk[rows, parity, :, 0, c * CH:(c + 1) * CH], ACT.Copy)
                act.activation(k_h[:], qk[:, parity, :, 1, c * CH:(c + 1) * CH], ACT.Copy).then_inc(pad_h_ready, 1)

            def ctx_split(chunk, c, from_bank):
                act.wait_ge(ctx_turned, chunk + 1)
                act.activation(ctx_h[:, c], from_bank[:, :].rearrange("p (k t) -> p k t", k=KC), ACT.Copy)\
                   .then_inc(ctx_h_ready, 1)

            def wqkv_high(k):
                act.wait_ge(wqkv_loaded[k], 16)
                part = slice(0, 2 * C)
                if k == KC:
                    k, part = slice(0, KC), slice(2 * C, 3 * C)
                act.activation(wqkv_h[:, k, part], stage_w[:, k, part], ACT.Copy).then_inc(wqkv_h_ready, 1)

            wqkv_high(0)
            act.wait_ge(cols_ready, 1)
            turn_in(0)
            for k in range(1, KC + 1):
                wqkv_high(k)
            act.wait_ge(bias_cols_loaded, 16)
            act.wait_ge(neg_ready, 1)
            for g in range(4):
                elu(0, g, g % 2)
            act.wait_ge(pad_h_cleared, 1)
            act.wait_ge(qk_ready, 4)
            spread_high(0, 0, 0)
            turn_in(1, bank[2:4])
            for u in range(2):
                k_in(0, u, bank[u], 0)

            def sum_wmod(s, cols):
                act.wait_ge(wmod_scaled, s - 2)
                for k in range(KC):
                    act.activation(stage_m2[:, s - 3, k], stage_m2[:, s - 3, k], ACT.Copy,
                                   accum_out=cols[:, k:k + 1]).then_inc(wmod_summed, 1)

            sum_wmod(3, mod_cols[:, 2 * KC:3 * KC])

            def step(i, half, parity, first, has_x, has_proj):
                if not first:
                    ctx_split(2 * i - 1, 1, ring[0])
                if has_proj:
                    elu(i + 1, 0, 1)
                act.wait_ge(scores_done, 8 * i + 4)
                spread_high(2 * i + 1, parity, 1)
                if has_proj:
                    elu(i + 1, 1, 0)
                if first:
                    act.wait_ge(wout_scaled, 1)
                    act.activation(wout_h[:], stage_m2[:, 2], ACT.Copy).then_inc(wout_h_ready, 1)
                    sum_wmod(4, mod_cols[:, 3 * KC:4 * KC])
                if has_proj:
                    elu(i + 1, 2, 1)
                    elu(i + 1, 3, 0)
                    k_in(i + 1, 0, ring[0], 1 - parity)
                if has_proj:
                    act.wait_ge(scores_done, 8 * i + 8)
                    act.wait_ge(qk_ready, 4 * i + 8)
                    spread_high(2 * i + 2, 1 - parity, 0)
                if not has_proj:
                    for k in range(KC - 1):
                        turn_in_block0(k)
                ctx_split(2 * i, 0, ring[1])
                if not has_proj:
                    turn_in_block0(KC - 1)
                if has_proj:
                    k_in(i + 1, 1, ring[0], 1 - parity)
                if has_x:
                    turn_in(i + 2)
                if first:
                    sum_wmod(5, gates[:, 1])

            def turn_in_block0(k):
                act.wait_ge(f_turned, k + 1)
                if k == 0:
                    act.wait_ge(piece_read, 2 * NB)
                else:
                    act.wait_ge(f_l, k)
                act.activation(gf_first[:], ring[0][:], ACT.Identity, bias=mod_cols[:, 2 * KC + k:2 * KC + k + 1],
                               scale=mod_cols[:, 3 * KC + k:3 * KC + k + 1]).then_inc(f_mod, 1)

            phase1_blocks(act, step)

            def f_turn_in(b, pair):
                for k in (2 * pair, 2 * pair + 1):
                    act.wait_ge(f_turned, KC * b + k + 1)
                    act.wait_ge(f_l, KC * b + k - 1)
                    act.activation(gf[:, k % 2], bank[turn_bank[k]][:], ACT.Identity,
                                   bias=mod_cols[:, 2 * KC + k:2 * KC + k + 1],
                                   scale=mod_cols[:, 3 * KC + k:3 * KC + k + 1]).then_inc(f_mod, 1)

            def silu(b, k):
                act.wait_ge(gu_done, KF * b + k + 1)
                if not (isinstance(b, int) and b == 0 and k < 2):
                    act.wait_ge(hid_ready, KF * b + k - 1)
                act.activation(sil[:, k % 2], bank[4 + 2 * (k % 2)][:], ACT.Silu, scale=W_SCALE)\
                   .then_inc(sil_ready, 1)

            def hid_split(b, k):
                act.wait_ge(hid_ready, KF * b + k + 1)
                if not (isinstance(b, int) and b == 0 and k < 4):
                    act.wait_ge(down_k, KF * b + k - 3)
                act.activation(hid_h[:, k % 4], hid[:, k % 2], ACT.Copy).then_inc(hid_h_ready, 1)

            def fstep(b, half, parity, first, has_next):
                silu(b, 0)
                if first:
                    ctx_split(2 * NB - 1, 1, bank[2])
                for k in range(KF):
                    if k == TURN_AT and has_next:
                        f_turn_in(b + 1, 0)
                        f_turn_in(b + 1, 1)
                    if k + 1 < KF:
                        silu(b, k + 1)
                    hid_split(b, k)

            phase2_blocks(act, fstep)

        @block.vector
        def _(dve):
            def normalise(m, loads, parity):
                dve.wait_ge(x_loaded[parity], 16 * loads)
                for t in range(2):
                    dve.bn_stats(bn[:, t], xb[:, parity, t]).then_inc(bn_done, 1)
                dve.wait_ge(bn_done, 2 * m + 2)
                dve.memset(wait_pad[:], 0.0)
                for t in range(2):
                    dve.bn_aggr(mean_var[:, t], bn[:, t]).then_inc(stats_ready, 1)

            def normalise2(m, parity):
                dve.wait_ge(rstd_ready, m + 1)
                if not (isinstance(m, int) and m == 0):
                    dve.wait_ge(x_turned, 2 * m)
                for t in range(2):
                    dve.tensor_scalar(xn[:, t], xb[:, parity, t], mean_var[:, t, 0:1], rstd[:, t:t + 1],
                                      ALU.subtract, ALU.mult).then_inc(xn_ready, 1)

            def split_h(m):
                if not (isinstance(m, int) and m == 0):
                    dve.wait_ge(v_done, 2 * m)
                for u in range(2):
                    k = slice(2 * u, 2 * u + 2)
                    dve.wait_ge(hf_ready, 4 * m + 2 * u + 2)
                    dve.tensor_copy(hh[:, k], hf[:, k]).then_inc(hh_ready, 1)
                    dve.wait_ge(hh_ready, 2 * m + u + 1)
                    dve.tensor_tensor(hl[:, k], hf[:, k], hh[:, k].bitcast(F32), ALU.subtract).then_inc(hl_ready, 1)

            def elu_sum(n, g, parity):
                dve.wait_ge(elu_parts, 4 * n + g + 1)
                dve.tensor_tensor(qk[:, parity, g], e_part[:, g % 2], r_part[:, g % 2], ALU.add)\
                   .then_inc(qk_ready, 1)

            def values(n, c, parity, b):
                dve.wait_ge(v_done, 2 * n + c + 1)
                dve.tensor_tensor(v_rows[:, parity, c].rearrange("p (h e) -> p h e", e=HV)[:, :, 0:HD],
                                  ring[b][:, :].rearrange("p (h e) -> p h e", e=HD),
                                  bv_rows[:].rearrange("p (h e) -> p h e", e=HD), ALU.add).then_inc(v_ready, 1)

            def mask_scores(chunk):
                for n, g in enumerate(SCORE_ORDER):
                    dve.wait_ge(scores_done, 4 * chunk + n + 1)
                    dve.tensor_tensor(masked[:, g], bank[g][:, :].rearrange("p (j t) -> p j t", j=HG),
                                      causal[:].unsqueeze(1).broadcast_to((P, HG, CH)), ALU.mult)\
                       .then_inc(masked_ready, 1)

            def spread_low(chunk, parity, c):
                dve.wait_ge(pad_h_ready, chunk + 1)
                for j in range(HG):
                    rows = slice(HD * j, HD * (j + 1))
                    dve.tensor_tensor(qpad_l[rows, :, j], qk[rows, parity, :, 0, c * CH:(c + 1) * CH],
                                      qpad_h[rows, :, j].bitcast(F32), ALU.subtract)
                dve.tensor_tensor(k_l[:], qk[:, parity, :, 1, c * CH:(c + 1) * CH], k_h[:].bitcast(F32),
                                  ALU.subtract).then_inc(pad_l_ready, 1)

            def context(chunk):
                dve.wait_ge(context_done, chunk + 1)
                half_h = H // 2
                for u in range(2):
                    rows = bank[u][:, 0:half_h * HV].rearrange("p (h e) -> p h e", e=HV)
                    last = dve.tensor_scalar(den[:, u * half_h:(u + 1) * half_h], rows[:, :, HD], ATTN_EPS, None, ALU.add)
                last.then_inc(den_ready, 1)
                dve.wait_ge(den_ready, chunk + 1)
                dve.reciprocal(rden[:], den[:]).then_inc(rden_ready, 1)
                dve.wait_ge(rden_ready, chunk + 1)
                if not (isinstance(chunk, int) and chunk == 0):
                    dve.wait_ge(ctx_turned, chunk)
                for u in range(2):
                    rows = bank[u][:, 0:half_h * HV].rearrange("p (h e) -> p h e", e=HV)
                    last = dve.tensor_tensor(
                        ctx_rows[:, u * half_h * HD:(u + 1) * half_h * HD].rearrange("p (h e) -> p h e", e=HD),
                        rows[:, :, 0:HD],
                        rden[:, u * half_h:(u + 1) * half_h].unsqueeze(2).broadcast_to((P, half_h, HD)), ALU.mult)
                last.then_inc(ctx_ready, 1)

            def mask_state():
                for u in range(2):
                    last = dve.tensor_tensor(state[:, 2 * u:2 * u + 2],
                                             state_bank[u][:, 0:2 * GV].rearrange("p (g e) -> p g e", g=2),
                                             head_mask[:].unsqueeze(1).broadcast_to((P, 2, GV)), ALU.mult)
                last.then_inc(state_ready, 1)

            def ctx_low(chunk, c, from_bank):
                dve.wait_ge(ctx_h_ready, chunk + 1)
                dve.tensor_tensor(ctx_l[:, c], from_bank[:, :].rearrange("p (k t) -> p k t", k=KC),
                                  ctx_h[:, c].bitcast(F32), ALU.subtract).then_inc(ctx_l_ready, 1)

            def add_residual(chunk, c, from_bank):
                dve.wait_ge(out_done, chunk + 1)
                dve.wait_ge(xres_ready, chunk + 1)
                dve.tensor_tensor(xres[:, c], from_bank[:], xres[:, c], ALU.add).then_inc(x1_ready, 1)

            def piece_range(i):
                dve.wait_ge(ends_ready, 2 * i + 1)
                dve.wait_ge(piece_loaded, 16 * i + 16)
                dve.tensor_reduce(piece_ends[:, 0:1], piece[:], AX, ALU.max).then_inc(piece_read, 1)
                dve.tensor_reduce(piece_ends[:, 1:2], piece[:], AX, ALU.min).then_inc(piece_read, 1)
                dve.wait_ge(piece_read, 2 * i + 2)
                dve.tensor_tensor(w_ends[:, 0:1], w_ends[:, 0:1], piece_ends[:, 0:1], ALU.max).then_inc(ends_ready, 1)
                dve.tensor_tensor(w_ends[:, 1:2], w_ends[:, 1:2], piece_ends[:, 1:2], ALU.min).then_inc(ends_ready, 1)

            def weights_held():
                dve.wait_ge(ends_ready, 2 * NB + 1)
                dve.tensor_scalar(w_held[:, 0:1], w_ends[:, 0:1], W_HELD, None, ALU.is_le).then_inc(bounds_ready, 1)
                dve.tensor_scalar(w_held[:, 1:2], w_ends[:, 1:2], -W_HELD, None, ALU.is_ge).then_inc(bounds_ready, 1)
                dve.wait_ge(bounds_ready, 2)
                dve.tensor_tensor(w_held[:, 2:3], w_held[:, 0:1], w_held[:, 1:2], ALU.mult).then_inc(held_ready, 1)

            def f_stats_of(b, loads, parity):
                dve.wait_ge(x1_loaded[parity], 16 * loads)
                for t in range(NT):
                    dve.bn_stats(bn[:, t], x1b[parity][:, t]).then_inc(f_bn, 1)
                dve.wait_ge(f_bn, NT * b + NT)
                dve.memset(wait_pad[:], 0.0)
                for t in range(NT):
                    dve.bn_aggr(mean_var[:, t], bn[:, t]).then_inc(f_stats, 1)

            def f_normalise(b, parity):
                dve.wait_ge(f_rstd, b + 1)
                if isinstance(b, int) and b == 0:
                    dve.wait_ge(x_turned, 2 * NB)
                    dve.wait_ge(hl_ready, 2 * NB)
                else:
                    dve.wait_ge(f_turned, KC * b)
                for t in range(NT):
                    dve.tensor_scalar(x1n[:, t], x1b[parity][:, t], mean_var[:, t, 0:1], rstd[:, t:t + 1],
                                      ALU.subtract, ALU.mult).then_inc(f_norm, 1)

            steps = [0]

            def link(ins):
                steps[0] += 1
                ins.then_inc(setup_step, 1)
                dve.wait_ge(setup_step, steps[0])

            link(dve.memset(head_mask[:], 0.0))
            dve.memset(w_ends[:], 0.0).then_inc(ends_ready, 1)
            for j in range(HG):
                last = dve.memset(head_mask[HD * j:HD * j + HD, HV * j:HV * j + HV], 1.0)
            link(last)

            def modulate(s, wm, cols):
                dve.wait_ge(wmod_loaded[s], 16)
                for k in range(KC):
                    link(dve.scalar_tensor_tensor(out=products[:], in0=wm(k), scalar=1.0, in1=silu_rows[:],
                                                  op0=ALU.mult, op1=ALU.mult, accum_out=cols[:, k:k + 1]))

            def gate(i):
                g, sgn, mag = gates[:, i], gates[:, 2], gates[:, 3]
                link(dve.tensor_scalar(sgn, g, 0.0, 2.0, ALU.is_ge, ALU.mult))
                link(dve.tensor_scalar(sgn, sgn, -1.0, None, ALU.add))
                link(dve.tensor_scalar(mag, g, -1.0, 0.25, ALU.mult, ALU.max))
                link(dve.tensor_tensor(mag, g, mag, ALU.max))
                return dve.tensor_tensor(g, sgn, mag, ALU.mult)

            def wqkv_low(k):
                dve.wait_ge(wqkv_h_ready, k + 1)
                part = slice(0, 2 * C)
                if k == KC:
                    k, part = slice(0, KC), slice(2 * C, 3 * C)
                dve.tensor_tensor(wqkv_l[:, k, part], stage_w[:, k, part], wqkv_h[:, k, part].bitcast(F32), ALU.subtract)\
                   .then_inc(wqkv_ready, 1)

            normalise(0, 1, 0)
            dve.wait_ge(silu_ready, 1)
            modulate(0, lambda k: stage_m[:, 0, k], mod_cols[:, 0:KC])
            normalise2(0, 0)
            modulate(1, lambda k: stage_m[:, 1, k], mod_cols[:, KC:2 * KC])
            dve.tensor_scalar(mod_cols[:, KC:2 * KC], mod_cols[:, KC:2 * KC], 1.0, None, ALU.add)\
               .then_inc(cols_ready, 1)
            wqkv_low(0)
            split_h(0)
            wqkv_low(2)
            wqkv_low(3)
            dve.wait_ge(bias_cols_loaded, 16)
            dve.tensor_scalar(neg_bqk_cols[:], bqk_cols[:], -1.0, None, ALU.mult).then_inc(neg_ready, 1)
            normalise(1, 1, 1)
            wqkv_low(KC)
            normalise2(1, 1)
            modulate(2, lambda k: stage_m[:, 0, k], gates[:, 0])
            gate(0).then_inc(gates_ready, 1)
            elu_sum(0, 0, 0)
            elu_sum(0, 1, 0)
            dve.memset(qpad_h[:].bitcast(F32), 0.0).then_inc(pad_h_cleared, 1)
            elu_sum(0, 2, 0)
            dve.wait_ge(state_zeroed, 1)
            mask_state()
            elu_sum(0, 3, 0)
            dve.wait_ge(pad_l_cleared, 1)
            spread_low(0, 0, 0)
            dve.wait_ge(bias_rows_loaded, 32)
            values(0, 0, 0, 0)
            values(0, 1, 0, 1)
            split_h(1)
            dve.wait_ge(gates_loaded, 16)
            dve.wait_ge(wout_loaded, 16)
            dve.tensor_tensor(stage_m2[:, 2], stage_m2[:, 2], ga_rows.unsqueeze(1).broadcast_to((P, KC, C)), ALU.mult)\
               .then_inc(wout_scaled, 1)
            dve.tensor_tensor(gab_rows[:], gab_rows[:], ga_rows, ALU.mult).then_inc(gab_ready, 1)
            dve.wait_ge(gab_ready, 1)

            def wout_low():
                dve.wait_ge(wout_h_ready, 1)
                dve.tensor_tensor(wout_l[:], stage_m2[:, 2], wout_h[:].bitcast(F32), ALU.subtract)\
                   .then_inc(wout_ready, 1)

            def finish_modulation():
                dve.wait_ge(wmod_summed, 3 * KC)
                link(dve.tensor_scalar(mod_cols[:, 3 * KC:4 * KC], mod_cols[:, 3 * KC:4 * KC], 1.0, None, ALU.add))
                link(gate(1))
                dve.tensor_scalar(gates[:, 1], gates[:, 1], W_SCALE, W_SCALE, ALU.mult, ALU.mult)\
                   .then_inc(gates_ready, 1)

            def step(i, half, parity, first, has_x, has_proj):
                other = 1 - parity
                if not first:
                    ctx_low(2 * i - 1, 1, ring[0])
                mask_scores(2 * i)
                if has_proj:
                    elu_sum(i + 1, 0, other)
                spread_low(2 * i + 1, parity, 1)
                if has_proj:
                    elu_sum(i + 1, 1, other)
                if first:
                    wout_low()
                if has_x:
                    normalise(i + 2, half + 2, parity)
                elif has_proj:
                    f_stats_of(0, 1, 0)
                piece_range(i)
                if not has_proj:
                    weights_held()
                if has_proj:
                    elu_sum(i + 1, 2, other)
                context(2 * i)
                if has_proj:
                    elu_sum(i + 1, 3, other)
                dve.wait_ge(state_done, 2 * i + 1)
                mask_state()
                if not first:
                    add_residual(2 * i - 1, 1, ring[1])
                if not has_proj:
                    split_block0(0)
                mask_scores(2 * i + 1)
                if has_x:
                    normalise2(i + 2, parity)
                elif has_proj:
                    f_normalise(0, 0)
                else:
                    split_block0(1)
                    split_block0(2)
                if has_proj:
                    values(i + 1, 0, other, 1)
                    values(i + 1, 1, other, 0)
                ctx_low(2 * i, 0, ring[1])
                if has_proj:
                    spread_low(2 * i + 2, other, 0)
                if not has_proj:
                    copy_count()
                    split_block0(3)
                add_residual(2 * i, 0, ring[1])
                context(2 * i + 1)
                if has_proj and not has_x:
                    finish_modulation()
                if has_x:
                    split_h(i + 2)
                if has_proj:
                    dve.wait_ge(state_done, 2 * i + 2)
                    mask_state()

            def split_block0(k):
                if k == 0:
                    dve.wait_ge(v_done, 2 * NB)
                    dve.wait_ge(qk_ready, 4 * NB)
                high, low = g_hl[0]
                dve.wait_ge(f_mod, k + 1)
                dve.tensor_copy(high[:, k], gf_first[:]).then_inc(f_h, 1)
                dve.wait_ge(f_h, k + 1)
                dve.tensor_tensor(low[:, k], gf_first[:], high[:, k].bitcast(F32), ALU.subtract).then_inc(f_l, 1)

            def copy_count():
                dve.wait_ge(count_done, 1)
                dve.tensor_copy(count[0:1, :], state_bank[0][0:1, 0:1]).then_inc(count_ready, 1)

            phase1_blocks(dve, step)

            def f_split(b, parity, pair):
                high, low = g_hl[parity]
                if not (isinstance(b, int) and b == 1):
                    dve.wait_ge(gu_done, KF * (b - 1))
                for k in (2 * pair, 2 * pair + 1):
                    dve.wait_ge(f_mod, KC * b + k + 1)
                    dve.tensor_copy(high[:, k], gf[:, k % 2]).then_inc(f_h, 1)
                    dve.wait_ge(f_h, KC * b + k + 1)
                    dve.tensor_tensor(low[:, k], gf[:, k % 2], high[:, k].bitcast(F32), ALU.subtract)\
                       .then_inc(f_l, 1)

            def hidden(b, k):
                dve.wait_ge(sil_ready, KF * b + k + 1)
                if not (isinstance(b, int) and b == 0 and k < 2):
                    dve.wait_ge(hid_l_ready, KF * b + k - 1)
                dve.tensor_tensor(hid[:, k % 2], bank[5 + 2 * (k % 2)][:], sil[:, k % 2], ALU.mult)\
                   .then_inc(hid_ready, 1)

            def hid_low(b, k):
                dve.wait_ge(hid_h_ready, KF * b + k + 1)
                dve.tensor_tensor(hid_l[:, k % 4], hid[:, k % 2], hid_h[:, k % 4].bitcast(F32), ALU.subtract)\
                   .then_inc(hid_l_ready, 1)

            def scale_down(b):
                dve.wait_ge(down_k, KF * b + KF)
                if isinstance(b, int) and b == 0:
                    dve.wait_ge(gates_loaded, 32)
                else:
                    dve.wait_ge(y_stored, 16 * b)
                for t in range(NT):
                    dve.tensor_tensor(y[:, t], bank[t][:], gb_rows[:], ALU.mult).then_inc(scaled, 1)

            def add_x1(b, parity):
                for t in range(NT):
                    dve.wait_ge(scaled, NT * b + t + 1)
                    dve.tensor_tensor(y[:, t], y[:, t], x1b[parity][:, t], ALU.add).then_inc(y_ready, 1)

            def fstep(b, half, parity, first, has_next):
                other = 1 - parity
                hidden(b, 0)
                if first:
                    ctx_low(2 * NB - 1, 1, bank[2])
                for k in range(KF):
                    if k == TURN_AT and has_next:
                        f_split(b + 1, other, 0)
                        f_split(b + 1, other, 1)
                    if k + 1 < KF:
                        hidden(b, k + 1)
                    hid_low(b, k)
                    if k == 0 and first:
                        add_residual(2 * NB - 1, 1, bank[3])
                    if k == 0 and not first:
                        scale_down(b - 1)
                    if k == 1 and not first:
                        add_x1(b - 1, other)
                    if k == TURN_AT - 3 and has_next:
                        f_stats_of(b + 1, half + parity + 1, other)
                    if k == TURN_AT - 2 and has_next:
                        f_normalise(b + 1, other)

            phase2_blocks(dve, fstep)
            dve.wait_ge(y_stored, 16 * (NF - 1))
            for t in range(NT + 1):
                if t < NT:
                    dve.wait_ge(last_down, t + 1)
                    dve.tensor_tensor(y[:, t], bank[t][:], gb_rows[:], ALU.mult).then_inc(scaled, 1)
                if t > 0:
                    dve.wait_ge(scaled, NT * (NF - 1) + t)
                    dve.tensor_tensor(y[:, t - 1], y[:, t - 1], x1b[1][:, t - 1], ALU.add).then_inc(y_ready, 1)

        @block.tensor
        def _(pe):
            def turn_x(m, u, banks=ring):
                for q in range(2):
                    for t in range(2):
                        k = 2 * u + q
                        last = pe.transpose(banks[u][:, q * TB + t * P:q * TB + (t + 1) * P],
                                            xn[:, t, k * P:(k + 1) * P], ident[:])
                last.then_inc(x_turned, 1)

            hs = (hh, hl, hh)
            ws = (wqkv_h, wqkv_h, wqkv_l)

            def qk_matmul(g, d, b):
                s, r = d // 12, d % 12
                k, q = r // 3, r % 3
                last = pe.matmul(ring[b][:, s * TB:(s + 1) * TB], ws[q][:, k, s * C + g * P:s * C + (g + 1) * P],
                                 hs[q][:, k], start=(r == 0), stop=(r == 11))
                if d == 23:
                    last.then_inc(qk_done, 1)

            def v_matmul(c, d, b):
                k, q = d // 3, d % 3
                last = pe.matmul(ring[b][:, :], hs[q][:, k, c * CH:(c + 1) * CH], ws[q][:, k, 2 * C:3 * C],
                                 start=(d == 0), stop=(d == 11))
                if d == 11:
                    last.then_inc(v_done, 1)

            def turn_k(n, u, to_bank, parity):
                pe.wait_ge(qk_ready, 4 * n + 2 * u + 2)
                for q in range(2):
                    for c in range(2):
                        last = pe.transpose(to_bank[:, (2 * q + c) * P:(2 * q + c + 1) * P],
                                            qk[:, parity, 2 * u + q, 1, c * CH:(c + 1) * CH], ident[:])
                last.then_inc(k_turned, 1)

            def scores(chunk, places):
                for n in places:
                    g = SCORE_ORDER[n]
                    if n == 0:
                        pe.wait_ge(pad_l_ready, chunk + 1)
                    if n == 2 and not (isinstance(chunk, int) and chunk == 0):
                        pe.wait_ge(ctx_ready, chunk)
                    for q in range(3):
                        last = pe.matmul(bank[g][:], (k_h, k_h, k_l)[q][:, g],
                                         (qpad_h, qpad_l, qpad_h)[q][:, g].rearrange("p j t -> p (j t)"),
                                         start=(q == 0), stop=(q == 2))
                    last.then_inc(scores_done, 1)

            def from_state(chunk, parity, c):
                pe.wait_ge(masked_ready, 4 * chunk + 4)
                pe.wait_ge(state_ready, chunk + 1)
                for g in range(KC):
                    pe.matmul(bank[g // 2][:, (g % 2) * GV:(g % 2 + 1) * GV], qk[:, parity, g, 0, c * CH:(c + 1) * CH],
                              state[:, g], start=(g % 2 == 0), stop=False, skip_group_check=True)

            def context_matmul(chunk, parity, c, n):
                g, j = n // HG, n % HG
                u = n // (H // 2)
                at_col = (n % (H // 2)) * HV
                last = pe.matmul(bank[u][:, at_col:at_col + HV], masked[:, g, j], v_rows[:, parity, c, n * HV:(n + 1) * HV],
                                 start=False, stop=(n % (H // 2) == H // 2 - 1), skip_group_check=True)
                if n == H - 1:
                    last.then_inc(context_done, 1)

            def add_to_state(parity, c):
                for g in range(KC):
                    last = pe.matmul(state_bank[g // 2][:, (g % 2) * GV:(g % 2 + 1) * GV], k_rows[:, parity, c, g],
                                     v_rows[:, parity, c, g * GV:(g + 1) * GV], start=False, stop=True,
                                     skip_group_check=True)
                last.then_inc(state_done, 1)

            def turn_ctx(chunk, to_bank):
                pe.wait_ge(ctx_ready, chunk + 1)
                for k in range(KC):
                    last = pe.transpose(to_bank[:, k * P:(k + 1) * P], ctx_rows[:, k * P:(k + 1) * P], ident[:])
                last.then_inc(ctx_turned, 1)

            def out_matmul(c, d, to_bank):
                k, q = d // 3, d % 3
                last = pe.matmul(to_bank[:, :], (ctx_h, ctx_l, ctx_h)[q][:, c, k], (wout_h, wout_h, wout_l)[q][:, k],
                                 start=(d == 0), stop=(d == 11))
                if d == 11:
                    last.then_inc(out_done, 1)

            pe.wait_ge(consts_ready, 2)
            for u in range(2):
                last = pe.matmul(state_bank[u][:, 0:2 * GV], masked[:, 0, 0],
                                 masked[:, 0].rearrange("p j t -> p (j t)")[:, 0:2 * GV], start=True, stop=True)
            last.then_inc(state_zeroed, 1)
            pe.wait_ge(xn_ready, 2)
            turn_x(0, 0)
            turn_x(0, 1)
            pe.wait_ge(hl_ready, 2)
            pe.wait_ge(hf_ready, 4)
            for g in range(4):
                if g >= 2:
                    pe.wait_ge(qk_read, g - 1)
                for d in range(24):
                    if g == 0 and d < 12 and d % 3 == 0:
                        k = d // 3
                        if k == MID:
                            pe.wait_ge(wqkv_mid_ready, 1)
                        else:
                            pe.wait_ge(wqkv_ready, k + (k < MID))
                    qk_matmul(g, d, g % 2)
                if g == 3:
                    turn_k(0, 0, bank[0], 0)
                    pe.wait_ge(xn_ready, 4)
                    for u in range(2):
                        turn_x(1, u, bank[2:4])
            pe.wait_ge(wqkv_ready, KC)
            for c in range(2):
                pe.wait_ge(qk_read, 3 + c)
                for d in range(12):
                    v_matmul(c, d, c)
                if c == 0:
                    turn_k(0, 1, bank[1], 0)
            pe.wait_ge(k_rows_ready, 2)
            pe.wait_ge(hf_ready, 8)

            def step(i, half, parity, first, has_x, has_proj):
                n, other = i + 1, 1 - parity
                scores(2 * i, (0, 1))
                if not first:
                    if has_proj:
                        pe.wait_ge(hf_ready, 4 * n + 2)
                    else:
                        pe.wait_ge(k_rows_ready, 2 * i + 2)
                    turn_ctx(2 * i - 1, ring[0])
                scores(2 * i, (2, 3))
                if not has_proj:
                    pe.wait_ge(ctx_l_ready, 2 * i)
                    turn_block0(0)
                    pe.wait_ge(x1_ready, 2 * i - 1)
                    for d in range(12):
                        out_matmul(1, d, ring[1])
                if has_proj:
                    pe.wait_ge(hf_ready, 4 * n + 4)
                    for d in range(24):
                        if d in (0, 6):
                            pe.wait_ge(hl_ready, 2 * n + 1 + d // 6)
                        qk_matmul(0, d, 1)
                    if not first:
                        pe.wait_ge(ctx_l_ready, 2 * i)
                    for d in range(24):
                        qk_matmul(1, d, 0)
                from_state(2 * i, parity, 0)
                if has_proj:
                    pe.wait_ge(qk_read, 4 * n + 1)
                pe.wait_ge(v_ready, 2 * i + 1)
                for h in range(H):
                    context_matmul(2 * i, parity, 0, h)
                    if has_proj:
                        for d in range(h * 24 // H, (h + 1) * 24 // H):
                            qk_matmul(2, d, 1)
                if has_proj:
                    pe.wait_ge(qk_read, 4 * n + 2)
                    for d in range(24):
                        qk_matmul(3, d, 0)
                pe.wait_ge(k_rows_ready, 2 * i + 2)
                add_to_state(parity, 0)
                if has_proj and not first:
                    pe.wait_ge(ctx_l_ready, 2 * i)
                    pe.wait_ge(qk_read, 4 * n + 3)
                    for d in range(12):
                        out_matmul(1, d, ring[1])
                if not has_proj:
                    turn_block0(1)
                if has_proj:
                    pe.wait_ge(qk_read, 4 * n + 4)
                    turn_k(n, 0, ring[0], other)
                scores(2 * i + 1, (0, 1, 2, 3))
                if has_proj:
                    if first:
                        pe.wait_ge(qk_read, 4 * n + 3)
                    else:
                        pe.wait_ge(x1_ready, 2 * i)
                    for d in range(12):
                        v_matmul(0, d, 1)
                    pe.wait_ge(k_rows_ready, 2 * n + 1)
                    for d in range(12):
                        v_matmul(1, d, 0)
                    pe.wait_ge(v_ready, 2 * n + 1)
                else:
                    turn_block0(2)
                    pe.wait_ge(x1_ready, 2 * i)
                turn_ctx(2 * i, ring[1])
                from_state(2 * i + 1, parity, 1)
                if has_proj:
                    pe.wait_ge(v_ready, 2 * n + 2)
                    turn_k(n, 1, ring[0], other)
                else:
                    pe.wait_ge(held_ready, 1)
                    pe.matmul(state_bank[0][0:1, 0:1], w_held[:, 2:3], ones_row[:, 0:1], start=True, stop=True)\
                      .then_inc(count_done, 1)
                pe.wait_ge(v_ready, 2 * i + 2)
                if first:
                    pe.wait_ge(wout_ready, 1)
                for h in range(H):
                    context_matmul(2 * i + 1, parity, 1, h)
                    if h == 3:
                        pe.wait_ge(ctx_l_ready, 2 * i + 1)
                    if 3 <= h < 15:
                        out_matmul(0, h - 3, ring[1])
                    if h == 8 and not has_proj:
                        turn_block0(3)
                if has_proj:
                    add_to_state(parity, 1)
                if has_x:
                    pe.wait_ge(xn_ready, 2 * i + 6)
                    pe.wait_ge(k_rows_ready, 2 * n + 2)
                    turn_x(i + 2, 0)
                    pe.wait_ge(x1_ready, 2 * i + 1)
                    turn_x(i + 2, 1)

            def turn_block0(k):
                if k == 0:
                    pe.wait_ge(f_norm, NT)
                else:
                    pe.wait_ge(f_mod, k)
                for t in range(NT):
                    last = pe.transpose(ring[0][:, t * P:(t + 1) * P], x1n[:, t, k * P:(k + 1) * P], ident[:])
                last.then_inc(f_turned, 1)

            phase1_blocks(pe, step)

            def f_turn(b, pair):
                for k in (2 * pair, 2 * pair + 1):
                    for t in range(NT):
                        last = pe.transpose(bank[turn_bank[k]][:, t * P:(t + 1) * P], x1n[:, t, k * P:(k + 1) * P],
                                            ident[:])
                    last.then_inc(f_turned, 1)

            def ffn_products(weights, halves):
                w_gate, w_up, w_down = weights

                def gate_up(b, kf, parity):
                    for s, w in ((0, w_gate), (1, w_up)):
                        for k in range(KC):
                            for half in range(2):
                                last = pe.matmul(bank[4 + 2 * (kf % 2) + s][:], w[:, k, kf * P:(kf + 1) * P],
                                                 halves(g_hl[parity][half][:, k]), start=(k == 0 and half == 0),
                                                 stop=(k == KC - 1 and half == 1))
                    last.then_inc(gu_done, 1)

                def down(b, kf):
                    pe.wait_ge(hid_l_ready, KF * b + kf + 1)
                    for t in range(NT):
                        for half, hid_x in ((0, hid_h), (1, hid_l)):
                            last = pe.matmul(bank[t][:], halves(hid_x[:, kf % 4, t * P:(t + 1) * P]), w_down[:, kf],
                                             start=(kf == 0 and half == 0), stop=(kf == KF - 1 and half == 1))
                        if isinstance(b, int) and b == NF - 1 and kf == KF - 1:
                            last.then_inc(last_down, 1)
                    if not (isinstance(b, int) and b == NF - 1 and kf == KF - 1):
                        last.then_inc(down_k, 1)

                def fstep(b, half, parity, first, has_next):
                    if first:
                        pe.wait_ge(wg_loaded, 16)
                        pe.wait_ge(wu_loaded, 16)
                    pe.wait_ge(f_l, KC * b + KC)
                    for kf in range(KF):
                        if kf == TURN_AT + 1 and has_next:
                            pe.wait_ge(f_norm, NT * b + 2 * NT)
                            pe.wait_ge(hid_ready, KF * b + kf - 1)
                            f_turn(b + 1, 0)
                            down(b, kf - 2)
                            pe.wait_ge(hid_ready, KF * b + kf)
                            f_turn(b + 1, 1)
                            pe.wait_ge(f_mod, KC * b + KC + 2)
                        elif kf == TURN_AT + 2 and has_next:
                            pe.wait_ge(f_mod, KC * b + KC + 4)
                        elif not (first and kf < 2):
                            pe.wait_ge(hid_ready, KF * b + kf - 1)
                        if first and kf == 1:
                            pe.wait_ge(x1_ready, 2 * NB - 1)
                        gate_up(b, kf, parity)
                        if first and kf == 0:
                            turn_ctx(2 * NB - 1, bank[2])
                        if first and kf == 1:
                            pe.wait_ge(ctx_l_ready, 2 * NB)
                            for d in range(12):
                                out_matmul(1, d, bank[3])
                        if kf < 2 and not first:
                            down(b - 1, KF - 2 + kf)
                        if kf == 2:
                            if first:
                                pe.wait_ge(wd_loaded, 16)
                                pe.wait_ge(x1_ready, 2 * NB)
                            else:
                                pe.wait_ge(scaled, NT * b)
                        if kf >= 2 and not (kf == TURN_AT + 1 and has_next):
                            down(b, kf - 2)
                phase2_blocks(pe, fstep)
                down(NF - 1, KF - 2)
                down(NF - 1, KF - 1)

            pe.wait_ge(count_ready, 1)
            held = pe.value_load(count[0:1, 0:1], min_val=0, max_val=P)
            with pe.If(held == P):
                ffn_products((wg, wu, wd), lambda half: half)
            with pe.Else():
                pe.wait_ge(full_loaded, 48)
                ffn_products((wg_full, wu_full, wd_full), lambda half: half.bitcast(F32))


_IN_ORDER = ("x", "wqkv_t", "b_qk", "b_v", "wout_t", "b_out", "w_ffn", "c_in", "wmod_t")


def kernel(**inputs):
    import numpy as _np
    import concourse.bacc as _bacc
    from concourse import mybir as _mybir
    from concourse.bass_utils import run_bass_kernel_spmd as _run

    nc = _bacc.Bacc("TRN2", target_bir_lowering=False, num_devices=1)
    x = _np.asarray(inputs["L0_attn_x"])
    C = x.shape[2]
    b_qkv = _np.asarray(inputs["L0_attn_b_qkv"])
    laid = {
        "x": x.reshape(x.shape[1], x.shape[2]),
        "wqkv_t": _np.asarray(inputs["L0_attn_w_qkv"]).T,
        "b_qk": b_qkv[:2 * C].reshape(2 * C // P, P).T,
        "b_v": b_qkv[2 * C:],
        "wout_t": _np.asarray(inputs["L0_attn_w_out"]).T,
        "b_out": _np.asarray(inputs["L0_attn_b_out"]),
        "w_ffn": _np.concatenate([_np.asarray(inputs["L0_ffn_" + n]).T.reshape(-1)
                                  for n in ("w_gate", "w_up", "w_down")]),
        "c_in": _np.asarray(inputs["L0_c"]).reshape(C),
        "wmod_t": _np.asarray(inputs["L0_wmod"]).T,
    }
    arrays, args = {}, []
    for name in _IN_ORDER:
        a = _np.ascontiguousarray(laid[name])
        arrays[f"in_{name}"] = a
        args.append(nc.dram_tensor(f"in_{name}", a.shape, _mybir.dt.from_np(a.dtype), kind="ExternalInput").ap())
    out = nc.dram_tensor("out_x", laid["x"].shape, _mybir.dt.float32, kind="ExternalOutput").ap()
    adaln_block(nc, *args, out)
    r = _run(nc, [arrays], core_ids=[0])
    return r.results[0]["out_x"].reshape(x.shape)
```
